# Optimizing a Trainium2 kernel written in Bass

```python
import numpy as np
import jax
import jax.numpy as jnp

def _softmax(x, axis=-1):
    return jax.nn.softmax(x, axis=axis)

def _gelu(x):
    return jax.nn.gelu(x, approximate=True)

def _silu(x):
    return jax.nn.silu(x)

def _sigmoid(x):
    return jax.nn.sigmoid(x)

def _layernorm(x, axis=-1, eps=1e-05):
    m = jnp.mean(x, axis=axis, keepdims=True)
    v = jnp.var(x, axis=axis, keepdims=True)
    return (x - m) / jnp.sqrt(v + eps)

def _scatter_add(tgt, idx, src, axis=0):
    return tgt.at[idx].add(src)

def _segment_sum(src, seg, n):
    return jax.ops.segment_sum(src, seg, n)
kernel_name = 'mk_flamingo_gated_d2_seqx_r4_b571db'

def setup_inputs(seed: int=0):
    np.random.seed(seed)
    _w = jnp.asarray

    def _rec_inputs():
        import jax
        import jax.numpy as jnp
        _rk = jax.random.key(seed)
        x = -0.0005207 + 1.001 * jax.random.normal(jax.random.fold_in(_rk, 1), (8, 100, 1024), jnp.float32)
        _lenS = 100 - jax.random.randint(jax.random.fold_in(_rk, 7), (8,), 0, max(1, 100 // 4) + 1, jnp.int32)
        _lenS2 = 361 - jax.random.randint(jax.random.fold_in(_rk, 8), (8,), 0, max(1, 361 // 4) + 1, jnp.int32)
        _ctx_4096P = jax.random.normal(jax.random.fold_in(_rk, 11), (8, 16, 1024), jnp.float32)
        _ctx_4096c = jax.random.dirichlet(jax.random.fold_in(_rk, 511), 0.3 * jnp.ones((16,), jnp.float32), (8, 361))
        _ctx_4096t = jnp.einsum('bsk,bkd->bsd', _ctx_4096c, _ctx_4096P)
        _ctx_4096t = _ctx_4096t * jax.lax.rsqrt(jnp.mean(jnp.square(_ctx_4096t)) + 1e-12) * 0.953939
        ctx_4096 = -0.00010331 + 0.999899 * (_ctx_4096t + 0.3 * jax.random.normal(jax.random.fold_in(_rk, 611), (8, 361, 1024), jnp.float32))
        _validS = jnp.arange(100)[None, :] < _lenS[:, None]
        _validS2 = jnp.arange(361)[None, :] < _lenS2[:, None]
        _causal = jnp.tril(jnp.ones((100, 100), dtype=bool))
        mask_1x1xSxS2_ff0 = jnp.where(jnp.ones((1, 1, 100, 361), dtype=bool), 0.0, -1000000000.0).astype(jnp.float32)
        _g = jax.random.normal(jax.random.fold_in(_rk, 9001), (2, 2), jnp.float32)
        _g = jnp.sign(_g) * jnp.maximum(jnp.abs(_g), 1.0) + (_g == 0) * 1.0
        g_xattn = _g[0]
        g_ffn = _g[1]
        return (x, ctx_4096, mask_1x1xSxS2_ff0, g_xattn, g_ffn)
    x, ctx_4096, mask_1x1xSxS2_ff0, g_xattn, g_ffn = _rec_inputs()

    def _L0_xattn_setup():
        import jax, jax.numpy as jnp
        import numpy as np
        B, Q, D = (8, 64, 1024)
        CTX = 1024
        H, KV, HD = (16, 4, 96)
        G = H // KV
        key = jax.random.key(seed)
        ks = jax.random.split(key, 6)
        s = 0.02
        return {'latents': jax.random.normal(ks[0], (B, Q, D), jnp.float32), 'context': jax.random.normal(ks[1], (B, CTX, D), jnp.float32), 'Wq': jax.random.normal(ks[2], (H * HD, D), jnp.float32) * s, 'Wk': jax.random.normal(ks[3], (KV * HD, D), jnp.float32) * s, 'Wv': jax.random.normal(ks[4], (KV * HD, D), jnp.float32) * s, 'Wo': jax.random.normal(ks[5], (D, H * HD), jnp.float32) * s}
    _L0_xattn_all = _L0_xattn_setup()
    _L0_xattn_in = {k: v for k, v in _L0_xattn_all.items() if k in ('Wq', 'Wk', 'Wv', 'Wo')}
    del _L0_xattn_all

    def _L0_ffn_setup():
        import jax, jax.numpy as jnp
        import numpy as np
        import math
        E, DK, R = (8, 32, 16)
        SCALING = 16.0 / 16.0
        key = jax.random.key(seed)
        ks = jax.random.split(key, 7)
        Bt, S, Din, Dout = (4, 512, 1024, 1024)
        x = jax.random.normal(ks[0], (Bt, S, Din), jnp.float32)
        W = jax.random.normal(ks[1], (Dout, Din), jnp.float32) * 0.02
        b = jnp.zeros((Dout,), jnp.float32)
        Wq = jax.random.normal(ks[2], (E * DK, Din), jnp.float32) * 0.02
        Wk = jax.random.normal(ks[3], (E * DK, Din), jnp.float32) * 0.02
        A = jax.random.normal(ks[4], (E, R, Din), jnp.float32) * 0.02
        Bm = jax.random.normal(ks[5], (E, Dout, R), jnp.float32) * 0.02
        return {'x': x, 'W': W, 'b': b, 'Wq': Wq, 'Wk': Wk, 'A': A, 'Bm': Bm}
    _L0_ffn_all = _L0_ffn_setup()
    _L0_ffn_in = {k: v for k, v in _L0_ffn_all.items() if k in ('W', 'b', 'Wq', 'Wk', 'A', 'Bm')}
    del _L0_ffn_all

    def _L1_xattn_setup():
        import jax, jax.numpy as jnp
        import numpy as np
        B, Q, K, D = (1, 256, 1601, 1024)
        H, KVH, HD = (32, 8, 128)
        GROUPS = H // KVH
        EPS = 1e-05

        def _rmsnorm(x, w):
            xf = x.astype(jnp.float32)
            var = jnp.mean(xf * xf, axis=-1, keepdims=True)
            return (xf * jax.lax.rsqrt(var + EPS)).astype(x.dtype) * w
        key = jax.random.key(seed)
        ks = jax.random.split(key, 8)
        s = 0.02
        return {'hidden_states': jax.random.normal(ks[0], (B, Q, D), jnp.float32), 'cross_attention_states': jax.random.normal(ks[1], (B, K, D), jnp.float32), 'attention_mask': jnp.zeros((B, 1, Q, K), jnp.float32), 'Wq': jax.random.normal(ks[2], (H * HD, D), jnp.float32) * s, 'Wk': jax.random.normal(ks[3], (KVH * HD, D), jnp.float32) * s, 'Wv': jax.random.normal(ks[4], (KVH * HD, D), jnp.float32) * s, 'Wo': jax.random.normal(ks[5], (D, H * HD), jnp.float32) * s, 'q_norm_w': jnp.ones((HD,), jnp.float32), 'k_norm_w': jnp.ones((HD,), jnp.float32)}
    _L1_xattn_all = _L1_xattn_setup()
    _L1_xattn_in = {k: v for k, v in _L1_xattn_all.items() if k in ('Wq', 'Wk', 'Wv', 'Wo', 'q_norm_w', 'k_norm_w')}
    del _L1_xattn_all

    def _L1_ffn_setup():
        import jax, jax.numpy as jnp
        import numpy as np
        N_STREAMS = 4
        DIM = 256
        SINKHORN_ITERS = 50
        SINKHORN_TAU = 0.1
        RMS_EPS = 1.1920929e-07

        def sinkhorn_log(logits, num_iters=SINKHORN_ITERS, tau=SINKHORN_TAU):
            Z = logits / tau
            u0 = jnp.zeros(Z.shape[:-1], Z.dtype)
            v0 = jnp.zeros_like(u0)

            def step(carry, _):
                u, v = carry
                u = -jax.nn.logsumexp(Z + v[..., None, :], axis=-1)
                v = -jax.nn.logsumexp(Z + u[..., :, None], axis=-2)
                return ((u, v), None)
            (u, v), _ = jax.lax.scan(step, (u0, v0), None, length=num_iters)
            return jnp.exp(Z + u[..., :, None] + v[..., None, :])
        key = jax.random.key(seed)
        ks = jax.random.split(key, 6)
        B, T = (4, 512)
        n, C = (N_STREAMS, DIM)
        wd = n * C
        x = jax.random.normal(ks[0], (B, T, wd), dtype=jnp.float32)
        W_res = 0.01 * jax.random.normal(ks[1], (n * n, wd), dtype=jnp.float32)
        W_pre = 0.01 * jax.random.normal(ks[2], (n, wd), dtype=jnp.float32)
        W_post = 0.01 * jax.random.normal(ks[3], (n, wd), dtype=jnp.float32)
        H_res_base = jnp.full((n, n), -0.5, dtype=jnp.float32)
        H_res_base = H_res_base.at[jnp.arange(n), jnp.arange(n)].set(0.0)
        H_pre_base = jnp.zeros((n,), dtype=jnp.float32).at[0].set(1.0)
        H_post_base = jnp.zeros((n,), dtype=jnp.float32)
        gate = jnp.array([5.0], dtype=jnp.float32)
        W_branch = 1.0 / np.sqrt(C) * jax.random.normal(ks[4], (C, C), dtype=jnp.float32)
        return {'x': x, 'W_res': W_res, 'W_pre': W_pre, 'W_post': W_post, 'H_res_base': H_res_base, 'H_pre_base': H_pre_base, 'H_post_base': H_post_base, 'gate': gate, 'W_branch': W_branch}
    _L1_ffn_all = _L1_ffn_setup()
    _L1_ffn_in = {k: v for k, v in _L1_ffn_all.items() if k in ('W_res', 'W_pre', 'W_post', 'H_res_base', 'H_pre_base', 'H_post_base', 'gate', 'W_branch')}
    del _L1_ffn_all
    return {'x': x, 'ctx_4096': ctx_4096, 'mask_1x1xSxS2_ff0': mask_1x1xSxS2_ff0, 'g_xattn': g_xattn, 'g_ffn': g_ffn, 'L0_xattn_Wq': _L0_xattn_in['Wq'], 'L0_xattn_Wk': _L0_xattn_in['Wk'], 'L0_xattn_Wv': _L0_xattn_in['Wv'], 'L0_xattn_Wo': _L0_xattn_in['Wo'], 'L0_ffn_W': _L0_ffn_in['W'], 'L0_ffn_b': _L0_ffn_in['b'], 'L0_ffn_Wq': _L0_ffn_in['Wq'], 'L0_ffn_Wk': _L0_ffn_in['Wk'], 'L0_ffn_A': _L0_ffn_in['A'], 'L0_ffn_Bm': _L0_ffn_in['Bm'], 'L1_xattn_Wq': _L1_xattn_in['Wq'], 'L1_xattn_Wk': _L1_xattn_in['Wk'], 'L1_xattn_Wv': _L1_xattn_in['Wv'], 'L1_xattn_Wo': _L1_xattn_in['Wo'], 'L1_xattn_q_norm_w': _L1_xattn_in['q_norm_w'], 'L1_xattn_k_norm_w': _L1_xattn_in['k_norm_w'], 'L1_ffn_W_res': _L1_ffn_in['W_res'], 'L1_ffn_W_pre': _L1_ffn_in['W_pre'], 'L1_ffn_W_post': _L1_ffn_in['W_post'], 'L1_ffn_H_res_base': _L1_ffn_in['H_res_base'], 'L1_ffn_H_pre_base': _L1_ffn_in['H_pre_base'], 'L1_ffn_H_post_base': _L1_ffn_in['H_post_base'], 'L1_ffn_gate': _L1_ffn_in['gate'], 'L1_ffn_W_branch': _L1_ffn_in['W_branch']}

def reference(x, ctx_4096, mask_1x1xSxS2_ff0, g_xattn, g_ffn, L0_xattn_Wq, L0_xattn_Wk, L0_xattn_Wv, L0_xattn_Wo, L0_ffn_W, L0_ffn_b, L0_ffn_Wq, L0_ffn_Wk, L0_ffn_A, L0_ffn_Bm, L1_xattn_Wq, L1_xattn_Wk, L1_xattn_Wv, L1_xattn_Wo, L1_xattn_q_norm_w, L1_xattn_k_norm_w, L1_ffn_W_res, L1_ffn_W_pre, L1_ffn_W_post, L1_ffn_H_res_base, L1_ffn_H_pre_base, L1_ffn_H_post_base, L1_ffn_gate, L1_ffn_W_branch):
    import jax
    import jax.numpy as jnp

    def _L0_xattn_ref(latents, context, Wq, Wk, Wv, Wo):
        import jax, jax.numpy as jnp
        import numpy as np
        B, Q, D = (8, 64, 1024)
        CTX = 1024
        H, KV, HD = (16, 4, 96)
        G = H // KV
        b, q_len, _ = latents.shape
        hidden = jnp.concatenate([context, latents], axis=1)
        s_len = hidden.shape[1]
        q = (latents @ Wq.T).reshape(b, q_len, H, HD)
        k = (hidden @ Wk.T).reshape(b, s_len, KV, HD)
        v = (hidden @ Wv.T).reshape(b, s_len, KV, HD)
        q = q.transpose(0, 2, 1, 3).reshape(b, KV, G, q_len, HD)
        k = k.transpose(0, 2, 1, 3)
        v = v.transpose(0, 2, 1, 3)
        scale = 1.0 / jnp.sqrt(jnp.asarray(HD, q.dtype))
        scores = jnp.einsum('bkgqd,bksd->bkgqs', q, k) * scale
        attn = jax.nn.softmax(scores.astype(jnp.float32), axis=-1).astype(q.dtype)
        out = jnp.einsum('bkgqs,bksd->bkgqd', attn, v)
        out = out.reshape(b, H, q_len, HD).transpose(0, 2, 1, 3).reshape(b, q_len, H * HD)
        return out @ Wo.T

    def _L0_ffn_ref(x, W, b, Wq, Wk, A, Bm):
        import jax, jax.numpy as jnp
        import numpy as np
        import math
        E, DK, R = (8, 32, 16)
        SCALING = 16.0 / 16.0
        Bt, S, Din = x.shape
        result = jnp.einsum('bsi,oi->bso', x, W) + b
        q = jnp.einsum('bsi,ni->bsn', x, Wq).reshape(Bt, S, E, DK)
        k = jnp.einsum('bsi,ni->bsn', x, Wk).reshape(Bt, S, E, DK)
        scores = jnp.einsum('bsed,bsed->bse', q, k) / math.sqrt(DK)
        w = jax.nn.softmax(scores, axis=-1)
        h = jnp.einsum('bsi,eri->bser', x, A)
        combined = jnp.einsum('bse,bser,eor->bso', w, h, Bm) * SCALING
        return result + combined

    def _L1_xattn_ref(hidden_states, cross_attention_states, attention_mask, Wq, Wk, Wv, Wo, q_norm_w, k_norm_w):
        import jax, jax.numpy as jnp
        import numpy as np
        B, Q, K, D = (1, 256, 1601, 1024)
        H, KVH, HD = (32, 8, 128)
        GROUPS = H // KVH
        EPS = 1e-05

        def _rmsnorm(x, w):
            xf = x.astype(jnp.float32)
            var = jnp.mean(xf * xf, axis=-1, keepdims=True)
            return (xf * jax.lax.rsqrt(var + EPS)).astype(x.dtype) * w
        bsz, q_len, _ = hidden_states.shape
        kv_len = cross_attention_states.shape[1]
        q = (hidden_states @ Wq.T).reshape(bsz, q_len, H, HD).transpose(0, 2, 1, 3)
        k = (cross_attention_states @ Wk.T).reshape(bsz, kv_len, KVH, HD).transpose(0, 2, 1, 3)
        v = (cross_attention_states @ Wv.T).reshape(bsz, kv_len, KVH, HD).transpose(0, 2, 1, 3)
        q = _rmsnorm(q, q_norm_w)
        k = jnp.repeat(k, GROUPS, axis=1)
        v = jnp.repeat(v, GROUPS, axis=1)
        k = _rmsnorm(k, k_norm_w)
        scale = 1.0 / np.sqrt(HD)
        scores = jnp.einsum('bhqd,bhkd->bhqk', q, k) * scale
        scores = scores + attention_mask[:, :, :, :kv_len]
        probs = jax.nn.softmax(scores.astype(jnp.float32), axis=-1).astype(q.dtype)
        out = jnp.einsum('bhqk,bhkd->bhqd', probs, v)
        out = out.transpose(0, 2, 1, 3).reshape(bsz, q_len, H * HD)
        return out @ Wo.T

    def _L1_ffn_ref(x, W_res, W_pre, W_post, H_res_base, H_pre_base, H_post_base, gate, W_branch):
        import jax, jax.numpy as jnp
        import numpy as np
        N_STREAMS = 4
        DIM = 256
        SINKHORN_ITERS = 50
        SINKHORN_TAU = 0.1
        RMS_EPS = 1.1920929e-07

        def sinkhorn_log(logits, num_iters=SINKHORN_ITERS, tau=SINKHORN_TAU):
            Z = logits / tau
            u0 = jnp.zeros(Z.shape[:-1], Z.dtype)
            v0 = jnp.zeros_like(u0)

            def step(carry, _):
                u, v = carry
                u = -jax.nn.logsumexp(Z + v[..., None, :], axis=-1)
                v = -jax.nn.logsumexp(Z + u[..., :, None], axis=-2)
                return ((u, v), None)
            (u, v), _ = jax.lax.scan(step, (u0, v0), None, length=num_iters)
            return jnp.exp(Z + u[..., :, None] + v[..., None, :])
        B, T, nC = x.shape
        n = N_STREAMS
        C = nC // n
        x_norm = x * jax.lax.rsqrt(jnp.mean(x * x, axis=-1, keepdims=True) + RMS_EPS)
        H_res_logits = (x_norm @ W_res.T).reshape(B, T, n, n) + H_res_base
        H_pre_logits = x_norm @ W_pre.T + H_pre_base
        H_post_logits = x_norm @ W_post.T + H_post_base
        H_res = sinkhorn_log(H_res_logits)
        H_pre = jax.nn.softmax(H_pre_logits, axis=-1)
        H_post = jax.nn.softmax(H_post_logits, axis=-1)
        g = jax.nn.sigmoid(gate)[0]
        I = jnp.eye(n, dtype=H_res.dtype)
        H_res = (1.0 - g) * I + g * H_res
        x_streams = x.reshape(B, T, n, C)
        x_pre = jnp.einsum('btnc,btn->btc', x_streams, H_pre)
        y = x_pre @ W_branch
        x_mixed = jnp.einsum('btij,btjc->btic', H_res, x_streams)
        y_distributed = jnp.einsum('btc,btn->btnc', y, H_post)
        return (x_mixed + y_distributed).reshape(B, T, nC)
    x = x + jnp.tanh(g_xattn[0]) * _L0_xattn_ref(_layernorm(x, axis=-1), ctx_4096, L0_xattn_Wq, L0_xattn_Wk, L0_xattn_Wv, L0_xattn_Wo)
    x = x + jnp.tanh(g_ffn[0]) * _L0_ffn_ref(_layernorm(x, axis=-1), L0_ffn_W, L0_ffn_b, L0_ffn_Wq, L0_ffn_Wk, L0_ffn_A, L0_ffn_Bm)
    x = x + jnp.tanh(g_xattn[1]) * _L1_xattn_ref(_layernorm(x, axis=-1), ctx_4096, mask_1x1xSxS2_ff0, L1_xattn_Wq, L1_xattn_Wk, L1_xattn_Wv, L1_xattn_Wo, L1_xattn_q_norm_w, L1_xattn_k_norm_w)
    x = x + jnp.tanh(g_ffn[1]) * _L1_ffn_ref(_layernorm(x, axis=-1), L1_ffn_W_res, L1_ffn_W_pre, L1_ffn_W_post, L1_ffn_H_res_base, L1_ffn_H_pre_base, L1_ffn_H_post_base, L1_ffn_gate, L1_ffn_W_branch)
    return x

_drawn_inputs = setup_inputs


def setup_inputs(seed=0):
    import zlib

    import numpy as np

    out = dict(_drawn_inputs(seed))
    spreads = {'g_ffn': (-1.0, 0.2),
     'L0_ffn_b': (0.0, 0.1),
     'L1_xattn_q_norm_w': (1.0, 0.536),
     'L1_xattn_k_norm_w': (1.0, 0.597),
     'L1_ffn_H_post_base': (0.0, 0.371)}
    factors = {'L0_ffn_Wq': 8.0, 'L0_ffn_Wk': 8.0, 'L0_ffn_A': 4.204, 'L0_ffn_Bm': 4.199}
    for name, (base, spread) in spreads.items():
        noise = np.random.default_rng([zlib.crc32(name.encode()), seed]).standard_normal(out[name].shape)
        drawn = base * np.exp(spread * noise) if base else spread * noise
        out[name] = jnp.asarray(drawn.astype(out[name].dtype))
    for name, factor in factors.items():
        out[name] = (out[name] * factor).astype(out[name].dtype)
    return out
```

```python
from contextlib import ExitStack

import concourse.bass as bass
from concourse import mybir

F32 = mybir.dt.float32
F32R = mybir.dt.float32r
ALU = mybir.AluOpType
ACT = mybir.ActivationFunctionType
AX = mybir.AxisListType

P = 128
B, S, D = 8, 100, 1024
T = B * S
HT = T // 2
NC = D // P
KEYS = 361
KR, KC = 121, 3
CW = 364
G0, HD0 = 4, 96
G1, HD1 = 8, 128
HG = 4
KV0, KV1 = G0 * HD0, G1 * HD1
RMS_EPS = 1e-5
BANK = 512
BANKS = 4
FIRST = 1
DMA_FIRST = 16


def allocators(nc, stack, stage):
    def sb(name, shape, dtype=F32):
        return stack.enter_context(nc.sbuf_tensor(f"{stage}_{name}", shape, dtype))

    def ps(name, shape):
        return stack.enter_context(nc.psum_tensor(f"{stage}_{name}", shape, F32))

    sems = []

    def sem(name):
        sems.append(nc.alloc_semaphore(f"{stage}_{name}"))
        return sems[-1]

    def clear():
        if sems:
            nc.clear_and_free_semaphores(sems)
            nc.all_engine_barrier()

    stack.callback(clear)
    return sb, ps, sem


def real_rows(kc):
    return min(KR, KEYS - kc * KR)


def project_context_layer1(nc, io, scratch):
    HALF = KV1 // 2
    NGROUP = KC * 2
    HH = HALF // HD1
    RAW = 4
    EARLY = 4
    with ExitStack() as stack:
        sb, ps, sem = allocators(nc, stack, "context1")
        w_raw = sb("w_raw", [P, RAW, KV1])
        wk_hi = sb("wk_hi", [P, NC, KV1], F32R)
        wk_lo = sb("wk_lo", [P, NC, KV1], F32R)
        wv_hi = sb("wv_hi", [P, NC, KV1], F32R)
        wv_lo = sb("wv_lo", [P, NC, KV1], F32R)
        ctx_raw = sb("ctx_raw", [P, NC, CW])
        ctx_hi = sb("ctx_hi", [P, NC, CW], F32R)
        ctx_lo = sb("ctx_lo", [P, NC, CW], F32R)
        k_rows = sb("k_rows", [KR, KC, KV1])
        k_square = sb("k_square", [KR, HALF])
        k_sum = sb("k_sum", [KR, KC * G1])
        k_root = sb("k_root", [KR, KC * G1])
        k_scale = sb("k_scale", [KR, KC * G1])
        kt_out = sb("kt_out", [P, 2, KEYS])
        v_out = sb("v_out", [KR, 2, HALF])
        norm_w = sb("norm_w", [P, 2])
        norm_ww = sb("norm_ww", [P, 1])
        eps = sb("eps", [P, 1])
        ident = sb("ident", [P, P])
        one = sb("one", [P, 1])
        ps_rows = ps("ps_rows", [P, 4, BANK])
        ps_turn = ps("ps_turn", [P, 2, BANK])
        w_load0 = sem("w_load0")
        w_load1 = sem("w_load1")
        w_load2 = sem("w_load2")
        w_load3 = sem("w_load3")
        wk_hi_done = sem("wk_hi_done")
        wv_hi_done = sem("wv_hi_done")
        w_lo_done = sem("w_lo_done")
        ctx_load = sem("ctx_load")
        ctx_hi_done = sem("ctx_hi_done")
        ctx_lo_done = sem("ctx_lo_done")
        chunk_used = sem("chunk_used")
        norm_load = sem("norm_load")
        consts = sem("consts")
        ww_ready = sem("ww_ready")
        rows_done = sem("rows_done")
        bank_read = sem("bank_read")
        squared = sem("squared")
        summed = sem("summed")
        rooted = sem("rooted")
        scaled = sem("scaled")
        k_normed = sem("k_normed")
        turned = sem("turned")
        turn_read = sem("turn_read")
        kt_store0 = sem("kt_store0")
        kt_store1 = sem("kt_store1")
        v_store0 = sem("v_store0")
        v_store1 = sem("v_store1")
        block = stack.enter_context(nc.Block())
        w_load = [w_load0, w_load1, w_load2, w_load3]
        kt_store, v_store = [kt_store0, kt_store1], [v_store0, v_store1]
        NW = 2 * NC

        def wait_hi(engine, i):
            engine.wait_ge(wk_hi_done if i < NC else wv_hi_done, i % NC + 1)

        @block.sync
        def _(sp):
            for done in (*kt_store, *v_store):
                sp.sem_inc(done, DMA_FIRST)
            sp.dma_start(ctx_raw[:], io["ctxT"][0]).then_inc(ctx_load, 16)
            for i in range(NW):
                src = io["wk1T"] if i < NC else io["wv1T"]
                if i >= RAW:
                    wait_hi(sp, i - RAW)
                    sp.wait_ge(w_lo_done, i - RAW + 1)
                sp.dma_start(w_raw[:, i % RAW], src[i % NC]).then_inc(w_load[i % RAW], 16)
            sp.dma_start(norm_w[:, 0:1], io["qn"]).then_inc(norm_load, 16)
            sp.dma_start(norm_w[:, 1:2], io["kn"]).then_inc(norm_load, 16)

            def store_v(b, n):
                kc, half = n // 2, n % 2
                sp.wait_ge(bank_read, BANKS + b * 2 * NGROUP + NGROUP + n + 1)
                sp.dma_start(scratch["v1"][b, :, kc, half * HALF:(half + 1) * HALF],
                             v_out[:, n % 2]).then_inc(v_store[n % 2], 16)

            def stores(b):
                for n in range(EARLY):
                    store_v(b, n)
                for g in range(G1):
                    sp.wait_ge(turn_read, 2 + b * G1 + g + 1)
                    sp.dma_start(scratch["k1"][g, :, b, :], kt_out[:, g % 2]).then_inc(kt_store[g % 2], 16)
                for n in range(EARLY, NGROUP):
                    store_v(b, n)

            with sp.Fori(0, B - 1) as b:
                sp.wait_ge(ctx_hi_done, (b + 1) * NC)
                sp.wait_ge(ctx_lo_done, (b + 1) * NC)
                sp.dma_start(ctx_raw[:], io["ctxT"][b + 1]).then_inc(ctx_load, 16)
                stores(b)
            stores(B - 1)
            for s in range(2):
                sp.wait_ge(v_store[s], DMA_FIRST + 16 * B * NGROUP // 2)
                sp.wait_ge(kt_store[s], DMA_FIRST + 16 * B * G1 // 2)

        @block.gpsimd
        def _(pool):
            pool.memset(ident[:], 0.0).then_inc(consts, 1)
            pool.memset(eps[:], RMS_EPS).then_inc(consts, 1)
            pool.wait_ge(consts, 2)
            pool.affine_select(out=ident[:], in_=ident[:], compare_op=ALU.not_equal, fill=1.0,
                               base=0, pattern=[[-1, P]], channel_multiplier=1).then_inc(consts, 1)
            pool.memset(one[:], 1.0).then_inc(consts, 1)
            pool.wait_ge(consts, 4)
            for i in range(NC, NW):
                pool.wait_ge(w_load[i % RAW], 16 * (i // RAW + 1))
                pool.tensor_tensor(wv_hi[:, i % NC], w_raw[:, i % RAW], one[:].to_broadcast([P, KV1]), ALU.mult
                                   ).then_inc(wv_hi_done, 1)

        @block.scalar
        def _(act):
            def split_context(b, chunks):
                for c in chunks:
                    if c == 0:
                        act.wait_ge(ctx_load, (b + 1) * 16)
                    act.activation(ctx_hi[:, c], ctx_raw[:, c], ACT.Copy).then_inc(ctx_hi_done, 1)

            def split_next_context(b, chunks):
                for c in chunks:
                    if c < NC - 1:
                        act.wait_ge(chunk_used, b * (NC - 1) + c + 1)
                    else:
                        act.wait_ge(rows_done, FIRST + (b + 1) * 2 * NGROUP)
                    split_context(b + 1, (c,))

            def copy_v(b, n):
                act.wait_ge(rows_done, FIRST + b * 2 * NGROUP + NGROUP + n + 1)
                act.wait_ge(v_store[n % 2], DMA_FIRST + (b * (NGROUP // 2) + n // 2) * 16)
                act.activation(v_out[:, n % 2], ps_rows[:KR, (NGROUP + n) % 4], ACT.Copy).then_inc(bank_read, 1)

            def batch(b, next_batch):
                act.wait_ge(turned, FIRST + b * G1)
                for n in range(NGROUP):
                    act.wait_ge(rows_done, FIRST + b * 2 * NGROUP + n + 1)
                    act.activation(k_rows[:, n // 2, (n % 2) * HALF:(n % 2 + 1) * HALF],
                                   ps_rows[:KR, n % 4], ACT.Copy).then_inc(bank_read, 1)
                for n in range(EARLY):
                    copy_v(b, n)
                    if n == 1:
                        act.wait_ge(summed, FIRST + (b + 1) * NGROUP)
                        act.activation(k_root[:], k_sum[:], ACT.Sqrt, bias=eps[:KR], scale=1.0 / HD1
                                       ).then_inc(rooted, 1)
                for g in range(G1):
                    act.wait_ge(turned, FIRST + b * G1 + g + 1)
                    act.wait_ge(kt_store[g % 2], DMA_FIRST + (b * (G1 // 2) + g // 2) * 16)
                    act.activation(kt_out[:, g % 2], ps_turn[:, g % 2, :KEYS], ACT.Copy,
                                   scale=norm_ww[:]).then_inc(turn_read, 1)
                copy_v(b, NGROUP - 2)
                if next_batch:
                    split_next_context(b, range(NC - 1))
                copy_v(b, NGROUP - 1)
                if next_batch:
                    split_next_context(b, (NC - 1,))

            split_context(0, range(NC))
            for i in range(NC):
                act.wait_ge(w_load[i % RAW], 16 * (i // RAW + 1))
                act.activation(wk_hi[:, i], w_raw[:, i % RAW], ACT.Copy).then_inc(wk_hi_done, 1)
            act.wait_ge(consts, 4)
            act.sem_inc(bank_read, BANKS)
            act.sem_inc(turn_read, 2)
            act.sem_inc(rooted, FIRST)
            act.wait_ge(ww_ready, 1)
            with act.Fori(0, B - 1) as b:
                batch(b, True)
            batch(B - 1, False)

        @block.vector
        def _(dve):
            dve.sem_inc(summed, FIRST)
            def split_context(b):
                for c in range(NC):
                    dve.wait_ge(ctx_hi_done, b * NC + c + 1)
                    dve.tensor_tensor(ctx_lo[:, c], ctx_raw[:, c], ctx_hi[:, c].bitcast(F32),
                                      ALU.subtract).then_inc(ctx_lo_done, 1)

            def batch(b):
                dve.wait_ge(rooted, FIRST + b)
                for n in range(NGROUP):
                    kc, half = n // 2, n % 2
                    part = k_rows[:, kc, half * HALF:(half + 1) * HALF]
                    dve.wait_ge(bank_read, BANKS + b * 2 * NGROUP + n + 1)
                    dve.wait_ge(summed, FIRST + b * NGROUP + n)
                    dve.tensor_tensor(k_square[:], part, part, ALU.mult).then_inc(squared, 1)
                    dve.wait_ge(squared, b * NGROUP + n + 1)
                    at = kc * G1 + half * HH
                    dve.tensor_reduce(k_sum[:, at:at + HH], k_square[:].rearrange("p (h d) -> p h d", d=HD1),
                                      AX.X, ALU.add).then_inc(summed, 1)
                dve.wait_ge(rooted, FIRST + b + 1)
                dve.reciprocal(k_scale[:], k_root[:]).then_inc(scaled, 1)
                dve.wait_ge(scaled, b + 1)
                for kc in range(KC):
                    rows = k_rows[:, kc].rearrange("p (h d) -> p h d", d=HD1)
                    dve.tensor_tensor(rows, rows, k_scale[:, kc * G1:(kc + 1) * G1].unsqueeze(2)
                                      .to_broadcast([KR, G1, HD1]), ALU.mult).then_inc(k_normed, 1)

            split_context(0)
            for i in range(NW):
                hi, lo = (wk_hi, wk_lo) if i < NC else (wv_hi, wv_lo)
                wait_hi(dve, i)
                dve.tensor_tensor(lo[:, i % NC], w_raw[:, i % RAW], hi[:, i % NC].bitcast(F32),
                                  ALU.subtract).then_inc(w_lo_done, 1)
            dve.wait_ge(norm_load, 32)
            dve.tensor_tensor(norm_ww[:], norm_w[:, 0:1], norm_w[:, 1:2], ALU.mult).then_inc(ww_ready, 1)
            with dve.Fori(0, B - 1) as b:
                batch(b)
                split_context(b + 1)
            batch(B - 1)

        @block.tensor
        def _(pe):
            def rows(b, j, w_hi, w_lo, wait_weights):
                kc, half = (j % NGROUP) // 2, j % 2
                at, col = slice(kc * KR, (kc + 1) * KR), slice(half * HALF, (half + 1) * HALF)
                pe.wait_ge(bank_read, b * 2 * NGROUP + j + 1)
                for c in range(NC):
                    if j == 0:
                        pe.wait_ge(ctx_lo_done, b * NC + c + 1)
                    if wait_weights:
                        pe.wait_ge(w_lo_done, wait_weights + c)
                    for x, w in ((ctx_hi, w_hi), (ctx_hi, w_lo), (ctx_lo, w_hi)):
                        mm = pe.matmul(ps_rows[:KR, j % BANKS], x[:, c, at], w[:, c, col],
                                       start=(c == 0 and x is ctx_hi and w is w_hi),
                                       stop=(c == NC - 1 and x is ctx_lo))
                    if j == 2 * NGROUP - 1 and c < NC - 1:
                        mm.then_inc(chunk_used, 1)
                mm.then_inc(rows_done, 1)

            pe.sem_inc(rows_done, FIRST)
            pe.sem_inc(turned, FIRST)
            pe.wait_ge(consts, 4)
            with pe.Fori(0, B) as b:
                for j in range(NGROUP):
                    rows(b, j, wk_hi, wk_lo, 1 if j == 0 else 0)
                for j in range(NGROUP, NGROUP + EARLY):
                    rows(b, j, wv_hi, wv_lo, NC + 1 if j == NGROUP else 0)
                for g in range(G1):
                    pe.wait_ge(turn_read, b * G1 + g + 1)
                    for kc in range(KC):
                        if g == 0:
                            pe.wait_ge(k_normed, b * KC + kc + 1)
                        n = real_rows(kc)
                        turn = pe.transpose(ps_turn[:, g % 2, kc * KR:kc * KR + n],
                                            k_rows[:n, kc, g * HD1:(g + 1) * HD1], ident[:n, :n])
                    turn.then_inc(turned, 1)
                for j in range(NGROUP + EARLY, 2 * NGROUP):
                    rows(b, j, wv_hi, wv_lo, 0)


def layer_norm(nc, io, stage, tokens, ln_hi, ln_lo, load=False):
    with ExitStack() as stack:
        sb, ps, sem = allocators(nc, stack, stage)
        centred = sb("centred", [P, NC, T])
        square = sb("square", [P, NC, T])
        root = sb("root", [P, T])
        rstd = sb("rstd", [P, T])
        mean_w = sb("mean_w", [P, P])
        eps = sb("eps", [P, 1])
        ps_mean = ps("ps_mean", [P, 2, BANK])
        ps_var = ps("ps_var", [P, 2, BANK])
        load0 = sem("load0")
        load1 = sem("load1")
        consts = sem("consts")
        mean_done = sem("mean_done")
        centred_done = sem("centred_done")
        squared = sem("squared")
        var_done = sem("var_done")
        rooted = sem("rooted")
        rstd_done = sem("rstd_done")
        normed = sem("normed")
        hi_done = sem("hi_done")
        block = stack.enter_context(nc.Block())
        loads = [load0, load1]
        PAIRS = NC // 2

        def part(a, s, k):
            return a[:, 2 * k:2 * k + 2, s * HT:(s + 1) * HT]

        @block.sync
        def _(sp):
            if load:
                for s in range(2):
                    sp.dma_start(tokens[:, :, s * HT:(s + 1) * HT], io["xT"][:, :, s * HT:(s + 1) * HT]
                                 ).then_inc(loads[s], 16)

        @block.gpsimd
        def _(pool):
            pool.memset(mean_w[:], 1.0 / D).then_inc(consts, 1)
            pool.memset(eps[:], 1e-5).then_inc(consts, 1)

        @block.tensor
        def _(pe):
            pe.wait_ge(consts, 2)
            for s in range(2):
                if load:
                    pe.wait_ge(loads[s], 16)
                for c in range(NC):
                    mm = pe.matmul(ps_mean[:, s, :HT], mean_w[:], tokens[:, c, s * HT:(s + 1) * HT],
                                   start=(c == 0), stop=(c == NC - 1))
                mm.then_inc(mean_done, 1)
            for s in range(2):
                for c in range(NC):
                    pe.wait_ge(squared, s * PAIRS + c // 2 + 1)
                    mm = pe.matmul(ps_var[:, s, :HT], mean_w[:], square[:, c, s * HT:(s + 1) * HT],
                                   start=(c == 0), stop=(c == NC - 1))
                mm.then_inc(var_done, 1)

        @block.scalar
        def _(act):
            act.wait_ge(consts, 2)

            def squares(s):
                for k in range(PAIRS):
                    act.wait_ge(centred_done, s * PAIRS + k + 1)
                    act.activation(part(square, s, k), part(centred, s, k), ACT.Square).then_inc(squared, 1)

            def roots(s):
                act.wait_ge(var_done, s + 1)
                act.activation(root[:, s * HT:(s + 1) * HT], ps_var[:, s, :HT], ACT.Sqrt, bias=eps[:]
                               ).then_inc(rooted, 1)

            squares(0)
            squares(1)
            roots(0)
            roots(1)
            for s in range(2):
                for k in range(PAIRS):
                    act.wait_ge(normed, s * PAIRS + k + 1)
                    act.activation(part(ln_hi, s, k), part(centred, s, k), ACT.Copy).then_inc(hi_done, 1)

        @block.vector
        def _(dve):
            for s in range(2):
                dve.wait_ge(mean_done, s + 1)
                mean = ps_mean[:, s:s + 1, :HT].to_broadcast([P, 2, HT])
                for k in range(PAIRS):
                    dve.tensor_tensor(part(centred, s, k), part(tokens, s, k), mean, ALU.subtract
                                      ).then_inc(centred_done, 1)
            for s in range(2):
                at = slice(s * HT, (s + 1) * HT)
                dve.wait_ge(rooted, s + 1)
                dve.reciprocal(rstd[:, at], root[:, at]).then_inc(rstd_done, 1)
                dve.wait_ge(rstd_done, s + 1)
                dve.wait_ge(squared, (s + 1) * PAIRS)
                scale = rstd[:, at].unsqueeze(1).to_broadcast([P, 2, HT])
                for k in range(PAIRS):
                    dve.tensor_tensor(part(centred, s, k), part(centred, s, k), scale, ALU.mult
                                      ).then_inc(normed, 1)
            for s in range(2):
                for k in range(PAIRS):
                    dve.wait_ge(hi_done, s * PAIRS + k + 1)
                    dve.tensor_tensor(part(ln_lo, s, k), part(centred, s, k), part(ln_hi, s, k).bitcast(F32),
                                      ALU.subtract)


def project_layer0(nc, io, scratch, ln_hi, ln_lo):
    RING = 7
    KN = KEYS + 1
    XK, XV = 2 * G0, B
    with ExitStack() as stack:
        sb, ps, sem = allocators(nc, stack, "context0")
        w_raw = sb("w_raw", [P, 2, KV0])
        wk_hi = sb("wk_hi", [P, NC, KV0], F32R)
        wk_lo = sb("wk_lo", [P, NC, KV0], F32R)
        wv_hi = sb("wv_hi", [P, NC, KV0], F32R)
        wv_lo = sb("wv_lo", [P, NC, KV0], F32R)
        ctx_raw = sb("ctx_raw", [P, NC, CW])
        ctx_hi = sb("ctx_hi", [P, 2, NC, CW], F32R)
        ctx_lo = sb("ctx_lo", [P, 2, NC, CW], F32R)
        kt_out = sb("kt_out", [HD0, 2, HT])
        v_out = sb("v_out", [KR, 2, KV0])
        ps_out = ps("ps_out", [P, RING, BANK])
        w_load = [sem("w_load0"), sem("w_load1")]
        w_hi_done = sem("w_hi_done")
        w_lo_done = sem("w_lo_done")
        ctx_load = sem("ctx_load")
        ctx_hi_done = sem("ctx_hi_done")
        ctx_lo_done = sem("ctx_lo_done")
        group_done = sem("group_done")
        bank_read = sem("bank_read")
        kt_store = [sem("kt_store0"), sem("kt_store1")]
        v_store = [sem("v_store0"), sem("v_store1")]
        block = stack.enter_context(nc.Block())
        NW = 2 * NC

        def groups(j):
            return [(n, True, n, n % 2) for n in range(G0)] + \
                   [(G0 + kc, False, kc, (j * KC + kc) % 2) for kc in range(KC)]

        @block.sync
        def _(sp):
            for done in (*kt_store, *v_store):
                sp.sem_inc(done, DMA_FIRST)
            sp.dma_start(ctx_raw[:], io["ctxT"][0]).then_inc(ctx_load, 16)
            for i in range(NW):
                src = io["wk0T"] if i < NC else io["wv0T"]
                if i >= 2:
                    sp.wait_ge(w_lo_done, i - 1)
                sp.dma_start(w_raw[:, i % 2], src[i % NC]).then_inc(w_load[i % 2], 16)

            def load(b):
                sp.wait_ge(ctx_lo_done, b * NC)
                sp.dma_start(ctx_raw[:], io["ctxT"][b]).then_inc(ctx_load, 16)

            def stores(b, j):
                for n, is_k, i, slot in groups(j):
                    sp.wait_ge(bank_read, RING + b * RING + n + 1)
                    if is_k:
                        sp.dma_start(scratch["k0"][i, :, b, 0:KEYS], kt_out[:, slot, 0:KEYS]
                                     ).then_inc(kt_store[slot], 16)
                    else:
                        sp.dma_start(scratch["v0"][b, :, i, :], v_out[:, slot]).then_inc(v_store[slot], 16)

            with sp.Fori(0, B // 2 - 1) as i:
                for j in range(2):
                    load(2 * i + j + 1)
                    stores(2 * i + j, j)
            load(B - 1)
            stores(B - 2, 0)
            stores(B - 1, 1)
            for n in range(XK):
                g, s = n // 2, n % 2
                sp.wait_ge(bank_read, RING + B * RING + n + 1)
                sp.dma_start(scratch["k0"][g, :, s * B // 2:(s + 1) * B // 2, KEYS:KEYS + S],
                             kt_out[:, n % 2].rearrange("p (b t) -> p b t", t=S)).then_inc(kt_store[n % 2], 16)
            for b in range(XV):
                sp.wait_ge(bank_read, RING + B * RING + XK + b + 1)
                sp.dma_start(scratch["v0x"][b], v_out[:S, b % 2]).then_inc(v_store[b % 2], 16)
            for s in range(2):
                sp.wait_ge(kt_store[s], DMA_FIRST + 16 * (B * G0 + XK) // 2)
                sp.wait_ge(v_store[s], DMA_FIRST + 16 * (B * KC + XV) // 2)

        @block.scalar
        def _(act):
            for i in range(NW):
                dst = wk_hi if i < NC else wv_hi
                act.wait_ge(w_load[i % 2], 16 * (i // 2 + 1))
                act.activation(dst[:, i % NC], w_raw[:, i % 2], ACT.Copy).then_inc(w_hi_done, 1)
            act.sem_inc(bank_read, RING)
            with act.Fori(0, B // 2) as i:
                for j in range(2):
                    b = 2 * i + j
                    act.wait_ge(ctx_load, (b + 1) * 16)
                    act.wait_ge(group_done, (b + 1) * RING)
                    for c in range(NC):
                        act.activation(ctx_hi[:, j, c], ctx_raw[:, c], ACT.Copy).then_inc(ctx_hi_done, 1)
                    for n, is_k, k, slot in groups(j):
                        act.wait_ge(group_done, 2 * RING + b * RING + n + 1)
                        if is_k:
                            act.wait_ge(kt_store[slot], DMA_FIRST + (b * 2 + n // 2) * 16)
                            act.activation(kt_out[:, slot, 0:KEYS], ps_out[:HD0, n, 0:KEYS], ACT.Copy
                                           ).then_inc(bank_read, 1)
                        else:
                            act.wait_ge(v_store[slot], DMA_FIRST + (i * KC + (j * KC + k) // 2) * 16)
                            act.activation(v_out[:, slot], ps_out[:KR, n, 0:KV0], ACT.Copy).then_inc(bank_read, 1)
            for n in range(XK + XV):
                act.wait_ge(group_done, 2 * RING + B * RING + n + 1)
                bank = n % RING
                if n < XK:
                    act.wait_ge(kt_store[n % 2], DMA_FIRST + 16 * (B * G0 // 2 + n // 2))
                    act.activation(kt_out[:, n % 2], ps_out[:HD0, bank, 0:HT], ACT.Copy).then_inc(bank_read, 1)
                else:
                    b = n - XK
                    act.wait_ge(v_store[b % 2], DMA_FIRST + 16 * (B * KC // 2 + b // 2))
                    act.activation(v_out[:S, b % 2], ps_out[:S, bank, 0:KV0], ACT.Copy).then_inc(bank_read, 1)

        @block.vector
        def _(dve):
            for i in range(NW):
                hi, lo = (wk_hi, wk_lo) if i < NC else (wv_hi, wv_lo)
                dve.wait_ge(w_hi_done, i + 1)
                dve.tensor_tensor(lo[:, i % NC], w_raw[:, i % 2], hi[:, i % NC].bitcast(F32),
                                  ALU.subtract).then_inc(w_lo_done, 1)
            with dve.Fori(0, B // 2) as i:
                for j in range(2):
                    for c in range(NC):
                        dve.wait_ge(ctx_hi_done, (2 * i + j) * NC + c + 1)
                        dve.tensor_tensor(ctx_lo[:, j, c], ctx_raw[:, c], ctx_hi[:, j, c].bitcast(F32),
                                          ALU.subtract).then_inc(ctx_lo_done, 1)

        @block.tensor
        def _(pe):
            def product(out, left, right, wait=None):
                for c in range(NC):
                    if wait:
                        wait(c)
                    for a, b in ((0, 0), (0, 1), (1, 0)):
                        mm = pe.matmul(out, left[a](c), right[b](c), start=(c == 0 and a == b == 0),
                                       stop=(c == NC - 1 and a == 1))
                mm.then_inc(group_done, 1)

            pe.sem_inc(group_done, 2 * RING)
            with pe.Fori(0, B // 2) as i:
                for j in range(2):
                    b = 2 * i + j
                    for n, is_k, k, _ in groups(j):
                        pe.wait_ge(bank_read, b * RING + n + 1)

                        def wait(c, n=n, k=k, is_k=is_k, b=b):
                            if n == 0:
                                pe.wait_ge(ctx_lo_done, b * NC + c + 1)
                            if k == 0:
                                pe.wait_ge(w_lo_done, c + 1 + (0 if is_k else NC))
                        if is_k:
                            at = slice(k * HD0, (k + 1) * HD0)
                            product(ps_out[:HD0, n, 0:KN],
                                    (lambda c: wk_hi[:, c, at], lambda c: wk_lo[:, c, at]),
                                    (lambda c: ctx_hi[:, j, c, 0:KN], lambda c: ctx_lo[:, j, c, 0:KN]), wait)
                        else:
                            at = slice(k * KR, (k + 1) * KR)
                            product(ps_out[:KR, n, 0:KV0],
                                    (lambda c: ctx_hi[:, j, c, at], lambda c: ctx_lo[:, j, c, at]),
                                    (lambda c: wv_hi[:, c], lambda c: wv_lo[:, c]), wait)
            for n in range(XK + XV):
                pe.wait_ge(bank_read, B * RING + n + 1)
                if n < XK:
                    at, tk = slice(n // 2 * HD0, (n // 2 + 1) * HD0), slice(n % 2 * HT, (n % 2 + 1) * HT)
                    product(ps_out[:HD0, n % RING, 0:HT],
                            (lambda c: wk_hi[:, c, at], lambda c: wk_lo[:, c, at]),
                            (lambda c: ln_hi[:, c, tk], lambda c: ln_lo[:, c, tk]))
                else:
                    tk = slice((n - XK) * S, (n - XK + 1) * S)
                    product(ps_out[:S, n % RING, 0:KV0],
                            (lambda c: ln_hi[:, c, tk], lambda c: ln_lo[:, c, tk]),
                            (lambda c: wv_hi[:, c], lambda c: wv_lo[:, c]))


def attend(nc, io, scratch, tokens, ln_hi, ln_lo, layer):
    G, HD = (G0, HD0) if layer == 0 else (G1, HD1)
    ROWS = [real_rows(kc) for kc in range(KC)] + ([S] if layer == 0 else [])
    NK, NCH = sum(ROWS), len(ROWS)
    wq, wo = io["wq0"] if layer == 0 else io["wq1"], io["wo0"] if layer == 0 else io["wo1"]
    k_dram = scratch["k0"] if layer == 0 else scratch["k1"]
    v_dram = scratch["v0"] if layer == 0 else scratch["v1"]
    SCALE = float(HD) ** -0.5
    TILES = 8
    RAW, SPLIT = 2, 4
    QG, OG = 8, 16
    GEMMS = QG + OG
    AHEAD = 2
    P_SLOTS, KV_SLOTS = 3, 4
    KV_DMAS = 3 if layer == 0 else 2
    with ExitStack() as stack:
        sb, ps, sem = allocators(nc, stack, f"attend{layer}")
        w_raw = sb("w_raw", [P, RAW, D])
        w_hi = sb("w_hi", [P, SPLIT, D], F32R)
        w_lo = sb("w_lo", [P, SPLIT, D], F32R)
        q = sb("q", [HD, HG, T])
        o_hi = sb("o_hi", [HD, HG, T], F32R)
        o_lo = sb("o_lo", [HD, HG, T], F32R)
        k_in = sb("k_in", [HD, KV_SLOTS, NK])
        v_in = sb("v_in", [KR, KV_SLOTS, NCH, HD])
        p = sb("p", [S, P_SLOTS, HG, NK])
        pt = sb("pt", [KR, 2, NCH, HG * S])
        neg_max = sb("neg_max", [S, P_SLOTS, HG])
        exp_bias = sb("exp_bias", [S, P_SLOTS, HG])
        exp_sum = sb("exp_sum", [S, P_SLOTS, HG])
        exp_inv = sb("exp_inv", [S, P_SLOTS, HG])
        ident = sb("ident", [P, P])
        one = sb("one", [P, 1])
        gate_in = sb("gate_in", [P, 1])
        gate = sb("gate", [P, 1])
        if layer == 1:
            mask = sb("mask", [S, KEYS])
            q_square = sb("q_square", [HD, 2, HT])
            head_pick = sb("head_pick", [HD, HG, HG])
            q_sum = sb("q_sum", [HG, T])
            q_root = sb("q_root", [S, B, HG])
            q_scale = sb("q_scale", [S, B, HG])
            eps = sb("eps", [P, 1])
        ps_big = ps("ps_big", [P, BANKS, BANK])
        ps_turn = ps("ps_turn", [P, 2, BANK])
        ps_out = ps("ps_out", [P, BANK])
        ps_sum = ps("ps_sum", [P, BANK])
        w_load = [sem("w_load0"), sem("w_load1")]
        w_hi_done = sem("w_hi_done")
        w_lo_done = sem("w_lo_done")
        kv_load = [sem("kv_load0"), sem("kv_load1"), sem("kv_load2"), sem("kv_load3")]
        gemm_done = sem("gemm_done")
        q_read = sem("q_read")
        s_done = sem("s_done")
        s_read = sem("s_read")
        masked = sem("masked")
        maxed = sem("maxed")
        biased = sem("biased")
        exped = sem("exped")
        inverted = sem("inverted")
        p_ready = sem("p_ready")
        turned = sem("turned")
        turn_read = [sem("turn_read_act"), sem("turn_read_dve")]
        pv_done = sem("pv_done")
        o_hi_done = sem("o_hi_done")
        o_lo_done = sem("o_lo_done")
        o_read = sem("o_read")
        q_squared = sem("q_squared")
        q_summed = sem("q_summed")
        q_sum_copied = sem("q_sum_copied")
        r_turned = sem("r_turned")
        r_rooted = sem("r_rooted")
        r_ready = sem("r_ready")
        consts = sem("consts")
        side_load = sem("side_load")
        gated = sem("gated")
        block = stack.enter_context(nc.Block())
        PT_USED = KV_SLOTS - 1
        GEMM0 = 12 + FIRST

        def tile_free(g, t):
            return GEMM0 + g * GEMMS + 2 * (t - 3) if t >= HG else FIRST + g * GEMMS + 4 * t

        def slot_turned(g, b):
            return 2 * NCH + (g * B + max(b - P_SLOTS + 1, 0)) * NCH

        def w_view(w, slot, t):
            if t < HG:
                return w[:, slot, 0:NC * HD].rearrange("p (c n) -> p c n", c=NC)
            return w[:HD, slot].rearrange("p (h n) -> p h n", h=HG)

        def w_flat(w, slot, t):
            return w[:, slot, 0:NC * HD] if t < HG else w[:HD, slot]

        @block.sync
        def _(sp):
            sp.dma_start(gate_in[:], io["gx"][layer]).then_inc(side_load, 16)
            if layer == 1:
                sp.dma_start(mask[:], io["mask"]).then_inc(side_load, 16)

            def tile(g, t):
                sp.wait_ge(w_lo_done, g * TILES + t + 1)
                src = wq[g * HG + t] if t < HG else wo[g * HG + t - HG]
                sp.dma_start(w_flat(w_raw, t % RAW, t), src).then_inc(w_load[t % RAW], 16)

            def kv(g, b):
                sp.wait_ge(pv_done, g * B + b + 1)
                slot = b % KV_SLOTS
                done = kv_load[slot]
                sp.dma_start(k_in[:, slot], k_dram[g][:, b, :]).then_inc(done, 16)
                sp.dma_start(v_in[:, slot, 0:KC], v_dram[b][:, :, bass.ds(g * HD, HD)]).then_inc(done, 16)
                if layer == 0:
                    sp.dma_start(v_in[:S, slot, KC], scratch["v0x"][b][:, bass.ds(g * HD, HD)]).then_inc(done, 16)

            with sp.Fori(0, G) as g:
                tile(g, 0)
                tile(g, 1)
                for b in range(KV_SLOTS):
                    kv(g, b)
                for t in range(2, 6):
                    tile(g, t)
                for b in range(KV_SLOTS, B):
                    if b + 2 < TILES:
                        tile(g, b + 2)
                    kv(g, b)

        CONSTS = 9 if layer == 1 else 3

        @block.gpsimd
        def _(pool):
            pool.memset(ident[:], 0.0).then_inc(consts, 1)
            pool.wait_ge(consts, 1)
            pool.affine_select(out=ident[:], in_=ident[:], compare_op=ALU.not_equal, fill=1.0,
                               base=0, pattern=[[-1, P]], channel_multiplier=1).then_inc(consts, 1)
            if layer == 1:
                pool.memset(eps[:], RMS_EPS * HD).then_inc(consts, 1)
                pool.memset(head_pick[:], 0.0).then_inc(consts, 1)
                pool.wait_ge(consts, 4)
                for h in range(HG):
                    pool.memset(head_pick[:, h, h:h + 1], 1.0).then_inc(consts, 1)
            pool.memset(one[:], 1.0).then_inc(consts, 1)
            pool.wait_ge(consts, CONSTS)
            with pool.Fori(0, G) as g:
                for t in range(TILES):
                    pool.wait_ge(w_load[t % RAW], (g * (TILES // RAW) + t // RAW + 1) * 16)
                    pool.wait_ge(gemm_done, tile_free(g, t))
                    hi = w_flat(w_hi, t % SPLIT, t)
                    pool.tensor_tensor(hi, w_flat(w_raw, t % RAW, t), one[:hi.shape[0]].to_broadcast(hi.shape), ALU.mult
                                       ).then_inc(w_hi_done, 1)

        @block.scalar
        def _(act):
            act.wait_ge(side_load, 16 * (1 + layer))
            act.activation(gate[:], gate_in[:], ACT.Tanh).then_inc(gated, 1)
            act.wait_ge(consts, CONSTS)
            act.sem_inc(turn_read[0], 1)

            def exps(g, b, pair):
                act.wait_ge(biased if layer == 0 else maxed, 2 * (g * B + b) + pair + 1)
                if layer == 0 and pair == 0:
                    act.wait_ge(turned, slot_turned(g, b))
                slot = b % P_SLOTS
                for h in (2 * pair, 2 * pair + 1):
                    if layer == 0:
                        act.activation(p[:, slot, h], ps_big[:S, h, :NK], ACT.Exp, bias=exp_bias[:, slot, h:h + 1],
                                       scale=SCALE, accum_out=exp_sum[:, slot, h:h + 1]).then_inc(s_read, 1)
                    else:
                        act.activation(p[:, slot, h], p[:, slot, h], ACT.Exp, bias=neg_max[:, slot, h:h + 1],
                                       accum_out=exp_sum[:, slot, h:h + 1]).then_inc(exped, 1)

            with act.Fori(0, G) as g:
                act.wait_ge(s_done, FIRST + g * B * HG)
                for n in range(QG):
                    act.wait_ge(gemm_done, GEMM0 + g * GEMMS + n + 1)
                    if layer == 1:
                        if n >= 2:
                            act.wait_ge(q_summed, g * QG + n - 1)
                        act.activation(q_square[:, n % 2], ps_big[:HD, n % BANKS, :HT], ACT.Square).then_inc(q_squared, 1)
                    act.activation(q[:, n // 2, n % 2 * HT:(n % 2 + 1) * HT], ps_big[:HD, n % BANKS, :HT],
                                   ACT.Copy).then_inc(q_read, 1)
                if layer == 1:
                    for s in range(2):
                        act.wait_ge(q_summed, g * QG + QG)
                        act.activation(q_sum[:, s * HT:(s + 1) * HT], (ps_out, ps_sum)[s][:HG, :HT], ACT.Copy
                                       ).then_inc(q_sum_copied, 1)
                    act.wait_ge(r_turned, g + 1)
                    act.activation(q_root[:], ps_sum[:S, 0:B * HG].rearrange("p (b h) -> p b h", h=HG), ACT.Sqrt,
                                   bias=eps[:S]).then_inc(r_rooted, 1)
                exps(g, 0, 0)
                exps(g, 0, 1)
                exps(g, 1, 0)
                for b in range(B):
                    for kc in range(NCH):
                        i = b * NCH + kc
                        if i % 2 == 0:
                            act.wait_ge(turned, 2 * NCH + g * B * NCH + i + 1)
                            act.wait_ge(pv_done, PT_USED + g * B + b)
                            act.activation(pt[:ROWS[kc], b % 2, kc], ps_turn[:ROWS[kc], 0, :HG * S], ACT.Copy
                                           ).then_inc(turn_read[0], 1)
                    if b + 1 < B:
                        exps(g, b + 1, 1)
                    if b + AHEAD < B:
                        exps(g, b + AHEAD, 0)
                    act.wait_ge(pv_done, KV_SLOTS + g * B + b + 1)
                    if b == 0:
                        act.wait_ge(gemm_done, GEMM0 + g * GEMMS)
                    act.activation(o_hi[:, :, b * S:(b + 1) * S], ps_out[:HD, :HG * S].rearrange("p (h t) -> p h t", h=HG),
                                   ACT.Copy).then_inc(o_hi_done, 1)

        @block.vector
        def _(dve):
            dve.sem_inc(w_lo_done, RAW)
            dve.sem_inc(turn_read[1], 1)
            dve.sem_inc(o_read, BANKS)
            dve.sem_inc(o_lo_done, FIRST)
            dve.wait_ge(gated, 1)

            def split(g, t):
                dve.wait_ge(w_hi_done, g * TILES + t + 1)
                dve.tensor_tensor(w_flat(w_lo, t % SPLIT, t), w_flat(w_raw, t % RAW, t),
                                  w_flat(w_hi, t % SPLIT, t).bitcast(F32), ALU.subtract).then_inc(w_lo_done, 1)

            def maxima(g, b):
                slot = b % P_SLOTS
                for pair in range(2):
                    heads = slice(2 * pair, 2 * pair + 2)
                    if layer == 0:
                        dve.wait_ge(s_done, FIRST + g * B * HG + b * HG + heads.stop)
                        dve.tensor_reduce(neg_max[:, slot, heads], ps_big[:S, heads, :NK], AX.X, ALU.max, negate=True
                                          ).then_inc(maxed, 1)
                        dve.wait_ge(maxed, 2 * (g * B + b) + pair + 1)
                        dve.tensor_scalar(exp_bias[:, slot, heads], neg_max[:, slot, heads], SCALE, None, ALU.mult
                                          ).then_inc(biased, 1)
                        continue
                    if pair == 0:
                        dve.wait_ge(turned, slot_turned(g, b))
                    for h in (2 * pair, 2 * pair + 1):
                        dve.wait_ge(s_done, FIRST + g * B * HG + b * HG + h + 1)
                        dve.scalar_tensor_tensor(p[:, slot, h], ps_big[:S, h, :NK], q_scale[:, b, h:h + 1], mask[:],
                                                 ALU.mult, ALU.add).then_inc(s_read, 1)
                    dve.wait_ge(s_read, g * B * HG + b * HG + heads.stop)
                    dve.tensor_reduce(neg_max[:, slot, heads], p[:, slot, heads], AX.X, ALU.max, negate=True
                                      ).then_inc(maxed, 1)

            def normalise(g, b):
                slot = b % P_SLOTS
                dve.wait_ge(s_read if layer == 0 else exped, g * B * HG + (b + 1) * HG)
                dve.reciprocal(exp_inv[:, slot], exp_sum[:, slot]).then_inc(inverted, 1)
                dve.wait_ge(inverted, g * B + b + 1)
                for h in range(HG):
                    dve.tensor_scalar(p[:, slot, h], p[:, slot, h], exp_inv[:, slot, h:h + 1], None, ALU.mult
                                      ).then_inc(p_ready, 1)

            with dve.Fori(0, G) as g:
                for t in range(4):
                    split(g, t)
                if layer == 1:
                    dve.wait_ge(r_rooted, g + 1)
                    dve.reciprocal(q_scale[:], q_root[:]).then_inc(r_ready, 1)
                    dve.wait_ge(r_ready, g + 1)
                maxima(g, 0)
                maxima(g, 1)
                normalise(g, 0)
                for b in range(B):
                    if b < 4:
                        split(g, 4 + b)
                    for kc in range(NCH):
                        i = b * NCH + kc
                        if i % 2 == 1:
                            dve.wait_ge(turned, 2 * NCH + g * B * NCH + i + 1)
                            dve.wait_ge(pv_done, PT_USED + g * B + b)
                            dve.tensor_copy(pt[:ROWS[kc], b % 2, kc], ps_turn[:ROWS[kc], 1, :HG * S]
                                            ).then_inc(turn_read[1], 1)
                    if b + 1 < B:
                        normalise(g, b + 1)
                    if b + AHEAD < B:
                        maxima(g, b + AHEAD)
                    dve.wait_ge(o_hi_done, g * B + b + 1)
                    at = slice(b * S, (b + 1) * S)
                    dve.tensor_tensor(o_lo[:, :, at], ps_out[:HD, :HG * S].rearrange("p (h t) -> p h t", h=HG),
                                      o_hi[:, :, at].bitcast(F32), ALU.subtract).then_inc(o_lo_done, 1)
                for n in range(OG):
                    m, at = n // 2, slice(n % 2 * HT, (n % 2 + 1) * HT)
                    dve.wait_ge(gemm_done, GEMM0 + g * GEMMS + QG + n + 1)
                    dve.wait_ge(o_read, g * OG + n + 1)
                    dve.scalar_tensor_tensor(tokens[:, m, at], ps_big[:, n % BANKS, :HT], gate[:], tokens[:, m, at],
                                             ALU.mult, ALU.add).then_inc(o_read, 1)

        @block.tensor
        def _(pe):
            pe.sem_inc(gemm_done, GEMM0)
            pe.sem_inc(turned, 2 * NCH)
            pe.sem_inc(s_done, FIRST)
            pe.sem_inc(pv_done, KV_SLOTS)
            pe.wait_ge(consts, CONSTS)

            def product(out, chunks, left, right):
                for c in range(chunks):
                    for a, b in ((0, 0), (0, 1), (1, 0)):
                        mm = pe.matmul(out, left[a](c), right[b](c), start=(c == 0 and a == b == 0),
                                       stop=(c == chunks - 1 and a == 1))
                mm.then_inc(gemm_done, 1)

            def queries(g):
                for n in range(QG):
                    t, tk = n // 2, slice(n % 2 * HT, (n % 2 + 1) * HT)
                    if n % 2 == 0:
                        pe.wait_ge(w_lo_done, RAW + g * TILES + t + 1)
                    if n < BANKS:
                        pe.wait_ge(o_read, g * OG + n + 1)
                    else:
                        pe.wait_ge(q_read, g * QG + n - BANKS + 1)
                    hi, lo = w_view(w_hi, t % SPLIT, t), w_view(w_lo, t % SPLIT, t)
                    product(ps_big[:HD, n % BANKS, :HT], NC, (lambda c: hi[:, c], lambda c: lo[:, c]),
                            (lambda c: ln_hi[:, c, tk], lambda c: ln_lo[:, c, tk]))
                    if layer == 1 and n > 0:
                        sum_squares(g, n - 1)
                if layer == 1:
                    sum_squares(g, QG - 1)

            def turn_sums():
                for b in range(B):
                    turn = pe.transpose(ps_sum[:S, b * HG:(b + 1) * HG], q_sum[:, b * S:(b + 1) * S], ident[:HG, :HG])
                turn.then_inc(r_turned, 1)

            def sum_squares(g, n):
                h, s = n // 2, n % 2
                pe.wait_ge(q_squared, g * QG + n + 1)
                if n < 2:
                    pe.wait_ge(o_lo_done, FIRST + g * B)
                pe.matmul((ps_out, ps_sum)[s][:HG, :HT], head_pick[:, h], q_square[:, s], start=(h == 0),
                          stop=(h == HG - 1)).then_inc(q_summed, 1)

            def scores(g, b):
                for h in range(HG):
                    if b == 0:
                        pe.wait_ge(q_read, g * QG + QG)
                    else:
                        pe.wait_ge(s_read, g * B * HG + (b - 1) * HG + h + 1)
                    if h == 0:
                        pe.wait_ge(kv_load[b % KV_SLOTS], (g * (B // KV_SLOTS) + b // KV_SLOTS + 1) * 16 * KV_DMAS)
                    if layer == 1 and b == 0 and h == HG - 1:
                        pe.wait_ge(q_sum_copied, 2 * g + 2)
                    pe.matmul(ps_big[:S, h, :NK], q[:, h, b * S:(b + 1) * S], k_in[:, b % KV_SLOTS],
                              start=True, stop=True).then_inc(s_done, 1)

            def turns(g, b):
                at = 0
                for kc in range(NCH):
                    i = b * NCH + kc
                    pe.wait_ge(turn_read[i % 2], g * (B * NCH // 2) + i // 2 + 1)
                    for h in range(HG):
                        if kc == 0:
                            pe.wait_ge(p_ready, g * B * HG + b * HG + h + 1)
                        turn = pe.transpose(ps_turn[:ROWS[kc], i % 2, h * S:(h + 1) * S],
                                            p[:, b % P_SLOTS, h, at:at + ROWS[kc]], ident[:S, :S])
                    turn.then_inc(turned, 1)
                    at += ROWS[kc]

            def weigh_values(g, b):
                pe.wait_ge(o_lo_done, FIRST + g * B + b)
                if b == 0 and layer == 1:
                    pe.wait_ge(q_sum_copied, 2 * g + 2)
                for kc in range(NCH):
                    i = b * NCH + kc
                    pe.wait_ge(turn_read[i % 2], 1 + g * (B * NCH // 2) + i // 2 + 1)
                    mm = pe.matmul(ps_out[:HD, :HG * S], v_in[:ROWS[kc], b % KV_SLOTS, kc], pt[:ROWS[kc], b % 2, kc],
                                   start=(kc == 0), stop=(kc == NCH - 1))
                mm.then_inc(pv_done, 1)

            def outputs(g):
                for n in range(OG):
                    t, m, tk = HG + n // 4, n // 2, slice(n % 2 * HT, (n % 2 + 1) * HT)
                    if n % 4 == 0:
                        pe.wait_ge(w_lo_done, RAW + g * TILES + t + 1)
                    if n == 0:
                        pe.wait_ge(o_lo_done, FIRST + g * B + B)
                    if n < BANKS:
                        pe.wait_ge(s_read, g * B * HG + (B - 1) * HG + n + 1)
                    else:
                        pe.wait_ge(o_read, BANKS + g * OG + n - BANKS + 1)
                    hi, lo = w_view(w_hi, t % SPLIT, t), w_view(w_lo, t % SPLIT, t)
                    col = slice(m % 2 * P, (m % 2 + 1) * P)
                    product(ps_big[:, n % BANKS, :HT], HG, (lambda h: hi[:, h, col], lambda h: lo[:, h, col]),
                            (lambda h: o_hi[:, h, tk], lambda h: o_lo[:, h, tk]))

            with pe.Fori(0, G) as g:
                queries(g)
                scores(g, 0)
                if layer == 1:
                    turn_sums()
                scores(g, 1)
                for b in range(B):
                    turns(g, b)
                    if b + AHEAD < B:
                        scores(g, b + AHEAD)
                    weigh_values(g, b)
                outputs(g)


def feed_forward(nc, io, tokens, ln_hi, ln_lo):
    E, DK, R = 8, 32, 16
    EC = E * DK // P
    EXPERTS = P // DK
    QK, TILES = 2 * EC, 2 * EC + 1 + NC
    RAW, SPLIT = 2, 4
    HB = B // 2
    with ExitStack() as stack:
        sb, ps, sem = allocators(nc, stack, "ffn")
        w_raw = sb("w_raw", [P, RAW, NC, P])
        w_hi = sb("w_hi", [P, SPLIT, NC, P], F32R)
        w_lo = sb("w_lo", [P, SPLIT, NC, P], F32R)
        bm_raw = sb("bm_raw", [P, D])
        bm_hi = sb("bm_hi", [P, D], F32R)
        bm_lo = sb("bm_lo", [P, D], F32R)
        q = sb("q", [P, EC, T])
        qk = sb("qk", [P, EC, T])
        pick = sb("pick", [P, EC, E])
        neg_max = sb("neg_max", [S, B])
        shifted = sb("shifted", [S, B, E])
        weight = sb("weight", [S, B, E])
        total = sb("total", [S, B])
        inverse = sb("inverse", [S, B])
        spread = sb("spread", [S, B, E, R])
        h = sb("h", [P, T])
        wh = sb("wh", [P, T])
        wh_hi = sb("wh_hi", [P, T], F32R)
        wh_lo = sb("wh_lo", [P, T], F32R)
        ident = sb("ident", [P, P])
        one = sb("one", [P, 1])
        gate_in = sb("gate_in", [P, 1])
        gate = sb("gate", [P, 1])
        bias = sb("bias", [P, NC])
        gated_bias = sb("gated_bias", [P, NC])
        ps_big = ps("ps_big", [P, BANKS, BANK])
        ps_score = ps("ps_score", [P, BANK])
        ps_weight = ps("ps_weight", [P, 2, BANK])
        w_load = [sem("w_load0"), sem("w_load1")]
        side_load = sem("side_load")
        w_hi_done = sem("w_hi_done")
        w_lo_done = sem("w_lo_done")
        bm_hi_done = sem("bm_hi_done")
        bm_lo_done = sem("bm_lo_done")
        consts = sem("consts")
        gated = sem("gated")
        biased = sem("biased")
        gemm_done = sem("gemm_done")
        q_read = sem("q_read")
        k_read = sem("k_read")
        h_read = sem("h_read")
        o_read = sem("o_read")
        scored = sem("scored")
        softmax = sem("softmax")
        exped = sem("exped")
        weight_turned = sem("weight_turned")
        wh_done = sem("wh_done")
        wh_hi_done = sem("wh_hi_done")
        wh_lo_done = sem("wh_lo_done")
        block = stack.enter_context(nc.Block())

        def half(s):
            return slice(s * HT, (s + 1) * HT)

        @block.sync
        def _(sp):
            sp.dma_start(gate_in[:], io["gf"][0]).then_inc(side_load, 16)
            sp.dma_start(bias[:], io["bT"]).then_inc(side_load, 16)
            sp.dma_start(bm_raw[:], io["bmT"]).then_inc(side_load, 16)
            for t in range(TILES):
                sp.wait_ge(w_lo_done, t + 1)
                sp.dma_start(w_raw[:, t % RAW], io["wf"][t].rearrange("p (c n) -> p c n", c=NC)
                             ).then_inc(w_load[t % RAW], 16)

        @block.gpsimd
        def _(pool):
            pool.memset(ident[:], 0.0).then_inc(consts, 1)
            pool.memset(one[:], 1.0).then_inc(consts, 1)
            pool.memset(pick[:], 0.0).then_inc(consts, 1)
            pool.wait_ge(consts, 3)
            pool.affine_select(out=ident[:], in_=ident[:], compare_op=ALU.not_equal, fill=1.0,
                               base=0, pattern=[[-1, P]], channel_multiplier=1).then_inc(consts, 1)
            for c in range(EC):
                for e in range(EXPERTS):
                    at = c * EXPERTS + e
                    pool.wait_ge(consts, 4 + at)
                    pool.memset(pick[e * DK:(e + 1) * DK, c, at:at + 1], 1.0).then_inc(consts, 1)
            pool.wait_ge(consts, 4 + EC * EXPERTS)
            for t in range(TILES):
                pool.wait_ge(w_load[t % RAW], (t // RAW + 1) * 16)
                if t >= SPLIT:
                    pool.wait_ge(gemm_done, 2 * (t - SPLIT + 1))
                pool.tensor_tensor(w_hi[:, t % SPLIT], w_raw[:, t % RAW], one[:].unsqueeze(2).to_broadcast([P, NC, P]), ALU.mult).then_inc(w_hi_done, 1)

        @block.scalar
        def _(act):
            act.wait_ge(side_load, 48)
            act.activation(gate[:], gate_in[:], ACT.Tanh).then_inc(gated, 1)
            act.activation(bm_hi[:], bm_raw[:], ACT.Copy).then_inc(bm_hi_done, 1)
            for n in range(2 * EC):
                act.wait_ge(gemm_done, n + 1)
                act.activation(q[:, n // 2, half(n % 2)], ps_big[:, n % BANKS, :HT], ACT.Copy).then_inc(q_read, 1)
            for s in range(2):
                act.wait_ge(gemm_done, 2 * QK + s + 1)
                act.activation(h[:, half(s)], ps_big[:, (2 * QK + s) % BANKS, :HT], ACT.Copy).then_inc(h_read, 1)
            act.wait_ge(softmax, 2)
            act.activation(weight[:], shifted[:], ACT.Exp, scale=float(DK) ** -0.5).then_inc(exped, 1)
            for s in range(2):
                act.wait_ge(wh_done, s + 1)
                act.activation(wh_hi[:, half(s)], wh[:, half(s)], ACT.Copy).then_inc(wh_hi_done, 1)

        @block.vector
        def _(dve):
            dve.sem_inc(w_lo_done, RAW)

            def split(t):
                dve.wait_ge(w_hi_done, t + 1)
                dve.tensor_tensor(w_lo[:, t % SPLIT], w_raw[:, t % RAW], w_hi[:, t % SPLIT].bitcast(F32),
                                  ALU.subtract).then_inc(w_lo_done, 1)

            for t in range(SPLIT):
                split(t)
            dve.wait_ge(gated, 1)
            dve.tensor_scalar(gated_bias[:], bias[:], gate[:], None, ALU.mult).then_inc(biased, 1)
            dve.wait_ge(biased, 1)
            for m in range(NC):
                dve.tensor_scalar(tokens[:, m], tokens[:, m], gated_bias[:, m:m + 1], None, ALU.add).then_inc(biased, 1)
            dve.wait_ge(bm_hi_done, 1)
            dve.tensor_tensor(bm_lo[:], bm_raw[:], bm_hi[:].bitcast(F32), ALU.subtract).then_inc(bm_lo_done, 1)
            split(SPLIT)
            for n in range(2 * EC):
                if n == 2:
                    split(SPLIT + 1)
                dve.wait_ge(q_read, n + 1)
                dve.wait_ge(gemm_done, 2 * EC + n + 1)
                dve.tensor_tensor(qk[:, n // 2, half(n % 2)], ps_big[:, (2 * EC + n) % BANKS, :HT],
                                  q[:, n // 2, half(n % 2)], ALU.mult).then_inc(k_read, 1)
            dve.wait_ge(scored, 1)
            score = ps_score[:S, 0:B * E].rearrange("p (b e) -> p b e", e=E)
            dve.tensor_reduce(neg_max[:], score, AX.X, ALU.max, negate=True).then_inc(softmax, 1)
            dve.wait_ge(softmax, 1)
            dve.tensor_tensor(shifted[:], score, neg_max[:].unsqueeze(2).to_broadcast([S, B, E]), ALU.add
                              ).then_inc(softmax, 1)
            split(SPLIT + 2)
            dve.wait_ge(exped, 1)
            dve.tensor_reduce(total[:], weight[:], AX.X, ALU.add).then_inc(softmax, 1)
            dve.wait_ge(softmax, 3)
            dve.reciprocal(inverse[:], total[:]).then_inc(softmax, 1)
            dve.wait_ge(softmax, 4)
            dve.tensor_tensor(weight[:], weight[:], inverse[:].unsqueeze(2).to_broadcast([S, B, E]), ALU.mult
                              ).then_inc(softmax, 1)
            dve.wait_ge(softmax, 5)
            dve.tensor_copy(spread[:].rearrange("p b e r -> p (b e) r"),
                            weight[:].rearrange("p b e -> p (b e)").unsqueeze(2).to_broadcast([S, B * E, R])
                            ).then_inc(softmax, 1)
            for s in range(2):
                dve.wait_ge(weight_turned, s + 1)
                dve.wait_ge(h_read, s + 1)
                dve.tensor_tensor(wh[:, half(s)], ps_weight[:, s, :HT], h[:, half(s)], ALU.mult).then_inc(wh_done, 1)
            for s in range(2):
                dve.wait_ge(wh_hi_done, s + 1)
                dve.tensor_tensor(wh_lo[:, half(s)], wh[:, half(s)], wh_hi[:, half(s)].bitcast(F32), ALU.subtract
                                  ).then_inc(wh_lo_done, 1)
            dve.wait_ge(biased, 1 + NC)
            for n in range(2 * NC):
                if n % 2 == 0 and QK + 1 + n // 2 + 2 < TILES:
                    split(QK + 1 + n // 2 + 2)
                m, at = n // 2, half(n % 2)
                dve.wait_ge(gemm_done, 2 * (QK + 1) + n + 1)
                dve.scalar_tensor_tensor(tokens[:, m, at], ps_big[:, (2 * (QK + 1) + n) % BANKS, :HT], gate[:],
                                         tokens[:, m, at], ALU.mult, ALU.add).then_inc(o_read, 1)

        @block.tensor
        def _(pe):
            def product(t, n, extra=False):
                at, bank = half(n % 2), n % BANKS
                if n % 2 == 0:
                    pe.wait_ge(w_lo_done, RAW + t + 1)
                if n >= BANKS:
                    last = n - BANKS
                    if last < 2 * EC:
                        pe.wait_ge(q_read, last + 1)
                    elif last < 2 * QK:
                        pe.wait_ge(k_read, last - 2 * EC + 1)
                    elif last < 2 * QK + 2:
                        pe.wait_ge(h_read, last - 2 * QK + 1)
                    else:
                        pe.wait_ge(o_read, last - 2 * QK - 2 + 1)
                hi, lo = w_hi[:, t % SPLIT], w_lo[:, t % SPLIT]
                for c in range(NC):
                    for w, x in ((hi, ln_hi), (hi, ln_lo), (lo, ln_hi)):
                        mm = pe.matmul(ps_big[:, bank, :HT], w[:, c], x[:, c, at], start=(c == 0 and w is hi and x is ln_hi),
                                       stop=(c == NC - 1 and w is lo and not extra))
                if extra:
                    col = slice((t - QK - 1) * P, (t - QK) * P)
                    pe.wait_ge(wh_lo_done, n % 2 + 1)
                    pe.wait_ge(bm_lo_done, 1)
                    for w, x in ((bm_hi, wh_hi), (bm_hi, wh_lo), (bm_lo, wh_hi)):
                        mm = pe.matmul(ps_big[:, bank, :HT], w[:, col], x[:, at], start=False, stop=(w is bm_lo))
                mm.then_inc(gemm_done, 1)

            pe.wait_ge(consts, 4 + EC * EXPERTS)
            for t in range(QK + 1):
                for s in range(2):
                    product(t, 2 * t + s)
            pe.wait_ge(k_read, 2 * EC)
            for b in range(B):
                for c in range(EC):
                    mm = pe.matmul(ps_score[:S, b * E:(b + 1) * E], qk[:, c, b * S:(b + 1) * S], pick[:, c],
                                   start=(c == 0), stop=(c == EC - 1))
            mm.then_inc(scored, 1)
            pe.wait_ge(softmax, 6)
            for s in range(2):
                for b in range(HB):
                    turn = pe.transpose(ps_weight[:, s, b * S:(b + 1) * S],
                                        spread[:, s * HB + b].rearrange("p e r -> p (e r)"), ident[:S, :S])
                turn.then_inc(weight_turned, 1)
            for t in range(QK + 1, TILES):
                for s in range(2):
                    product(t, 2 * t + s, extra=True)


def mix_streams(nc, io, tokens, out):
    N, C = 4, D // 4
    CC = C // P
    NL = N * N + 2 * N
    TAU, ITERS, EPS_LN, EPS_RMS = 0.1, 50, 1e-5, 1.1920929e-07
    HB = B // 2
    BV = 5
    QUARTER = NC // 2
    with ExitStack() as stack:
        sb, ps, sem = allocators(nc, stack, "mix")
        x = sb("x", [S, B, D])
        y = sb("y", [S, B, D])
        yt = sb("yt", [P, NC, T])
        junk = sb("junk", [S, D])
        w = sb("w", [P, NC, NL])
        branch = sb("branch", [P, CC, C])
        base = sb("base", [S, NL])
        ident = sb("ident", [P, P])
        eye = sb("eye", [S, N, N])
        stats = sb("stats", [S, B, 2, 6])
        moments = sb("moments", [S, B, 2])
        eps = sb("eps", [S, 2])
        root = sb("root", [S, B])
        rstd = sb("rstd", [S, B])
        energy = sb("energy", [S, B])
        root2 = sb("root2", [S, B])
        rms = sb("rms", [S, B])
        logits_t = sb("logits_t", [NL, T])
        logits = sb("logits", [S, B, NL])
        io_max = sb("io_max", [S, B, 2])
        io_w = sb("io_w", [S, B, 2, N])
        io_sum = sb("io_sum", [S, B, 2])
        io_inv = sb("io_inv", [S, B, 2])
        out_w = sb("out_w", [S, B, N])
        z = sb("z", [S, B, N, N])
        h = sb("h", [S, B, N, N])
        side = sb("side", [S, B, N])
        side2 = sb("side2", [S, B, N])
        gates_in = sb("gates_in", [S, 2])
        gates = sb("gates", [S, 4])
        pre = sb("pre", [S, B, C])
        pre_t = sb("pre_t", [P, CC, T])
        deep = sb("deep", [S, B, C])
        part = sb("part", [S, 4, C])
        ps_turn = ps("ps_turn", [P, 4, BANK])
        ps_logits = ps("ps_logits", [P, 2, BANK])
        ps_rows = ps("ps_rows", [P, BANK])
        loads = sem("loads")
        consts = sem("consts")
        x_turned = sem("x_turned")
        x_copied = sem("x_copied")
        stat = sem("stat")
        moment = sem("moment")
        rooted = sem("rooted")
        rstd_done = sem("rstd_done")
        y_done = sem("y_done")
        energy_done = sem("energy_done")
        rooted2 = sem("rooted2")
        y_turned = sem("y_turned")
        yt_copied = sem("yt_copied")
        logits_done = sem("logits_done")
        logits_copied = sem("logits_copied")
        logits_turned = sem("logits_turned")
        gated = sem("gated")
        chain = sem("chain")
        io_exp = sem("io_exp")
        z_exp = sem("z_exp")
        z_ln = sem("z_ln")
        pre_done = sem("pre_done")
        pre_turned = sem("pre_turned")
        pre_copied = sem("pre_copied")
        deep_done = sem("deep_done")
        deep_copied = sem("deep_copied")
        part_done = sem("part_done")
        out_added = sem("out_added")
        mixed = sem("mixed")
        h_ready = sem("h_ready")
        stored = sem("stored")
        block = stack.enter_context(nc.Block())
        IO_SHIFTED, Z_SHIFTED = 5, 9

        @block.sync
        def _(sp):
            for dst, name in ((w, "wm"), (branch, "branch"), (base, "base"), (gates_in, "gates")):
                sp.dma_start(dst[:], io[name]).then_inc(loads, 16)
            for b in range(B):
                if b < BV:
                    sp.wait_ge(mixed, (b + 1) * N * N)
                else:
                    sp.wait_ge(out_added, B * N + (b + 1 - BV) * N * N)
                sp.dma_start(out[b], x[:, b]).then_inc(stored, 16)
            sp.wait_ge(stored, 16 * B)

        @block.gpsimd
        def _(pool):
            pool.memset(ident[:], 0.0).then_inc(consts, 1)
            pool.memset(eye[:], 0.0).then_inc(consts, 1)
            pool.memset(eps[:, 0:1], EPS_LN).then_inc(consts, 1)
            pool.memset(eps[:, 1:2], EPS_RMS).then_inc(consts, 1)
            pool.wait_ge(consts, 4)
            pool.affine_select(out=ident[:], in_=ident[:], compare_op=ALU.not_equal, fill=1.0,
                               base=0, pattern=[[-1, P]], channel_multiplier=1).then_inc(consts, 1)
            for i in range(N):
                pool.memset(eye[:, i, i:i + 1], 1.0).then_inc(consts, 1)
            for b in range(B):
                for i in range(N):
                    n = b * N + i
                    pool.wait_ge(part_done, n + 1)
                    pool.tensor_tensor(x[:, b, i * C:(i + 1) * C], x[:, b, i * C:(i + 1) * C], part[:, n % 4], ALU.add
                                       ).then_inc(out_added, 1)
            for n in range(B * N, B * N + (B - BV) * N * N):
                b, i = BV + (n - B * N) // (N * N), n % N
                pool.wait_ge(part_done, n + 1)
                pool.tensor_tensor(x[:, b, i * C:(i + 1) * C], x[:, b, i * C:(i + 1) * C], part[:, n % 4], ALU.add
                                   ).then_inc(out_added, 1)

        @block.tensor
        def _(pe):
            pe.wait_ge(consts, 5 + N)
            for b in range(B):
                for k in range(2):
                    n = 2 * b + k
                    if n >= 4:
                        pe.wait_ge(x_copied, n - 3)
                    for c in range(QUARTER):
                        turn = pe.transpose(ps_turn[:S, n % 4, c * P:(c + 1) * P],
                                            tokens[:, k * QUARTER + c, b * S:(b + 1) * S], ident[:])
                    turn.then_inc(x_turned, 1)
            for b in range(B):
                pe.wait_ge(y_done, b + 1)
                for k in range(2):
                    n = 2 * b + k
                    if n < 4:
                        pe.wait_ge(x_copied, 2 * B - 4 + n + 1)
                    else:
                        pe.wait_ge(yt_copied, n - 3)
                    for c in range(QUARTER):
                        at = (k * QUARTER + c) * P
                        turn = pe.transpose(ps_turn[:, n % 4, c * S:(c + 1) * S], y[:, b, at:at + P], ident[:S, :S])
                    turn.then_inc(y_turned, 1)
            pe.wait_ge(loads, 64)
            for s in range(2):
                pe.wait_ge(yt_copied, (s + 1) * B)
                for c in range(NC):
                    mm = pe.matmul(ps_logits[:NL, s, :HT], w[:, c], yt[:, c, s * HT:(s + 1) * HT],
                                   start=(c == 0), stop=(c == NC - 1))
                mm.then_inc(logits_done, 1)
            for s in range(2):
                pe.wait_ge(logits_copied, s + 1)
                for b in range(s * HB, (s + 1) * HB):
                    turn = pe.transpose(ps_rows[:S, b * NL:(b + 1) * NL], logits_t[:, b * S:(b + 1) * S], ident[:NL, :NL])
            turn.then_inc(logits_turned, 1)
            for b in range(B):
                pe.wait_ge(pre_done, b + 1)
                if b < 2:
                    pe.wait_ge(yt_copied, 2 * B)
                else:
                    pe.wait_ge(pre_copied, b - 1)
                for c in range(CC):
                    turn = pe.transpose(ps_turn[:, b % 2, c * S:(c + 1) * S], pre[:, b, c * P:(c + 1) * P], ident[:S, :S])
                turn.then_inc(pre_turned, 1)
                pe.wait_ge(pre_copied, b + 1)
                if b >= 2:
                    pe.wait_ge(deep_copied, b - 1)
                for c in range(CC):
                    mm = pe.matmul(ps_turn[:S, 2 + b % 2, :C], pre_t[:, c, b * S:(b + 1) * S], branch[:, c],
                                   start=(c == 0), stop=(c == CC - 1))
                mm.then_inc(deep_done, 1)

        @block.scalar
        def _(act):
            for b in range(B):
                for k in range(2):
                    n = 2 * b + k
                    act.wait_ge(x_turned, n + 1)
                    act.activation(x[:, b, k * BANK:(k + 1) * BANK], ps_turn[:S, n % 4], ACT.Copy).then_inc(x_copied, 1)
            act.wait_ge(consts, 5 + N)
            for s in range(2):
                bs = slice(s * HB, (s + 1) * HB)
                act.wait_ge(moment, (s + 1) * HB)
                act.activation(root[:, bs], moments[:, bs, 1], ACT.Sqrt, bias=eps[:, 0:1]).then_inc(rooted, 1)
            for b in range(B):
                act.wait_ge(y_done, b + 1)
                if b:
                    act.wait_ge(energy_done, b)
                act.activation(junk[:], y[:, b], ACT.Square, accum_out=energy[:, b:b + 1]).then_inc(energy_done, 1)
                for k in range(2):
                    n = 2 * b + k
                    act.wait_ge(y_turned, n + 1)
                    act.activation(yt[:, k * QUARTER:(k + 1) * QUARTER, b * S:(b + 1) * S],
                                   ps_turn[:, n % 4, :QUARTER * S].rearrange("p (c t) -> p c t", t=S), ACT.Copy
                                   ).then_inc(yt_copied, 1)
            act.wait_ge(energy_done, B)
            act.activation(root2[:], energy[:], ACT.Sqrt, scale=1.0 / D, bias=eps[:, 1:2]).then_inc(rooted2, 1)
            for s in range(2):
                act.wait_ge(logits_done, s + 1)
                act.activation(logits_t[:, s * HT:(s + 1) * HT], ps_logits[:NL, s, :HT], ACT.Copy).then_inc(logits_copied, 1)
            act.wait_ge(loads, 64)
            act.activation(gates[:, 0:1], gates_in[:, 0:1], ACT.Tanh).then_inc(gated, 1)
            act.activation(gates[:, 1:2], gates_in[:, 1:2], ACT.Exp, scale=-1.0).then_inc(gated, 1)
            act.wait_ge(chain, IO_SHIFTED)
            act.activation(io_w[:], io_w[:], ACT.Exp).then_inc(io_exp, 1)
            act.wait_ge(chain, Z_SHIFTED)
            act.activation(h[:], z[:], ACT.Exp).then_inc(z_exp, 1)
            act.wait_ge(chain, Z_SHIFTED + 1)
            act.activation(side2[:], side[:], ACT.Ln).then_inc(z_ln, 1)
            act.wait_ge(chain, Z_SHIFTED + 4)
            act.activation(h[:], z[:], ACT.Exp).then_inc(z_exp, 1)
            for b in range(B):
                act.wait_ge(pre_turned, b + 1)
                act.activation(pre_t[:, :, b * S:(b + 1) * S],
                               ps_turn[:, b % 2, :CC * S].rearrange("p (c t) -> p c t", t=S), ACT.Copy
                               ).then_inc(pre_copied, 1)
                act.wait_ge(deep_done, b + 1)
                act.activation(deep[:, b], ps_turn[:S, 2 + b % 2, :C], ACT.Copy).then_inc(deep_copied, 1)
                act.wait_ge(deep_copied, b + 1)
                for i in range(N):
                    n = b * N + i
                    if n >= 4:
                        act.wait_ge(out_added, n - 3)
                    act.activation(part[:, n % 4], deep[:, b], ACT.Copy, scale=out_w[:, b, i:i + 1]).then_inc(part_done, 1)
            act.wait_ge(h_ready, 1)
            n = B * N
            for b in range(BV, B):
                for j in range(N):
                    for i in range(N):
                        act.wait_ge(out_added, n - 3)
                        act.activation(part[:, n % 4], y[:, b, j * C:(j + 1) * C], ACT.Copy, scale=h[:, b, i, j:j + 1]
                                       ).then_inc(part_done, 1)
                        n += 1

        @block.vector
        def _(dve):
            for b in range(B):
                for k in range(2):
                    dve.wait_ge(x_copied, 2 * b + k + 1)
                    dve.bn_stats(stats[:, b, k], x[:, b, k * BANK:(k + 1) * BANK]).then_inc(stat, 1)
            for b in range(B):
                dve.wait_ge(stat, 2 * b + 2)
                dve.bn_aggr(moments[:, b], stats[:, b]).then_inc(moment, 1)
            for s in range(2):
                bs = slice(s * HB, (s + 1) * HB)
                dve.wait_ge(rooted, s + 1)
                dve.reciprocal(rstd[:, bs], root[:, bs]).then_inc(rstd_done, 1)
                dve.wait_ge(rstd_done, s + 1)
                dve.wait_ge(moment, (s + 1) * HB)
                for b in range(s * HB, (s + 1) * HB):
                    dve.tensor_scalar(y[:, b], x[:, b], moments[:, b, 0:1], rstd[:, b:b + 1], ALU.subtract, ALU.mult
                                      ).then_inc(y_done, 1)

            count = [0]

            def step(ins):
                count[0] += 1
                ins.then_inc(chain, 1)
                dve.wait_ge(chain, count[0])

            def rows(a):
                return a.unsqueeze(3).to_broadcast([S, B, N, N])

            def columns(a):
                return a.unsqueeze(2).to_broadcast([S, B, N, N])

            dve.wait_ge(rooted2, 1)
            step(dve.reciprocal(rms[:], root2[:]))
            dve.wait_ge(logits_turned, 1)
            dve.wait_ge(loads, 64)
            step(dve.tensor_tensor(logits[:], ps_rows[:S, 0:B * NL].rearrange("p (b l) -> p b l", l=NL),
                                   rms[:].unsqueeze(2).to_broadcast([S, B, NL]), ALU.mult))
            step(dve.tensor_tensor(logits[:], logits[:], base[:].unsqueeze(1).to_broadcast([S, B, NL]), ALU.add))
            io_logits = logits[:, :, N * N:NL].rearrange("p b (k n) -> p b k n", n=N)
            step(dve.tensor_reduce(io_max[:], io_logits, AX.X, ALU.max, negate=True))
            step(dve.tensor_tensor(io_w[:], io_logits, io_max[:].unsqueeze(3).to_broadcast([S, B, 2, N]), ALU.add))
            assert count[0] == IO_SHIFTED
            step(dve.tensor_scalar(z[:], logits[:, :, 0:N * N].rearrange("p b (i j) -> p b i j", j=N), 1.0 / TAU, None,
                                   ALU.mult))
            step(dve.tensor_reduce(side[:], z[:], AX.X, ALU.max, negate=True))
            dve.wait_ge(gated, 2)
            step(dve.tensor_scalar(gates[:, 2:3], gates[:, 1:2], 1.0, None, ALU.add))
            step(dve.tensor_tensor(z[:], z[:], rows(side[:]), ALU.add))
            assert count[0] == Z_SHIFTED
            dve.wait_ge(z_exp, 1)
            step(dve.tensor_reduce(side[:], h[:], AX.X, ALU.add))
            dve.wait_ge(z_ln, 1)
            step(dve.tensor_tensor(z[:], z[:], rows(side2[:]), ALU.subtract))
            step(dve.tensor_reduce(side[:], z[:].rearrange("p b i j -> p b j i"), AX.X, ALU.max, negate=True))
            step(dve.tensor_tensor(z[:], z[:], columns(side[:]), ALU.add))
            assert count[0] == Z_SHIFTED + 4
            dve.wait_ge(io_exp, 1)
            step(dve.tensor_reduce(io_sum[:], io_w[:], AX.X, ALU.add))
            step(dve.reciprocal(io_inv[:], io_sum[:]))
            step(dve.tensor_tensor(io_w[:], io_w[:], io_inv[:].unsqueeze(3).to_broadcast([S, B, 2, N]), ALU.mult))
            step(dve.tensor_scalar(out_w[:], io_w[:, :, 1], gates[:, 0:1], None, ALU.mult))
            for n in range(N):
                for b in range(B):
                    ins = y[:, b, n * C:(n + 1) * C]
                    if n == 0:
                        last = dve.tensor_scalar(pre[:, b], ins, io_w[:, b, 0, n:n + 1], None, ALU.mult)
                    else:
                        last = dve.scalar_tensor_tensor(pre[:, b], ins, io_w[:, b, 0, n:n + 1], pre[:, b], ALU.mult, ALU.add)
                    if n == N - 1:
                        last.then_inc(pre_done, 1)
                    elif b == B - 1:
                        step(last)

            def normalise(turned):
                view = h[:].rearrange("p b i j -> p b j i") if turned else h[:]
                step(dve.tensor_reduce(side[:], view, AX.X, ALU.add))
                step(dve.reciprocal(side2[:], side[:]))
                step(dve.tensor_tensor(h[:], h[:], (columns if turned else rows)(side2[:]), ALU.mult))

            dve.wait_ge(z_exp, 2)
            normalise(True)
            for _ in range(ITERS - 1):
                normalise(False)
                normalise(True)
            step(dve.reciprocal(gates[:, 3:4], gates[:, 2:3]))
            step(dve.tensor_scalar(h[:], h[:], gates[:, 3:4], gates[:, 0:1], ALU.mult, ALU.mult))
            step(dve.tensor_tensor(gates[:, 1:2], gates[:, 1:2], gates[:, 3:4], ALU.mult))
            step(dve.tensor_scalar(eye[:], eye[:], gates[:, 1:2], gates[:, 0:1], ALU.mult, ALU.mult))
            dve.tensor_tensor(h[:], h[:], eye[:].unsqueeze(1).to_broadcast([S, B, N, N]), ALU.add).then_inc(h_ready, 1)
            dve.wait_ge(h_ready, 1)
            for b in range(BV):
                for j in range(N):
                    for i in range(N):
                        n = (b * N + j) * N + i
                        if j == 0:
                            dve.wait_ge(out_added, b * N + i + 1)
                        else:
                            dve.wait_ge(mixed, n - N + 1)
                        at = slice(i * C, (i + 1) * C)
                        dve.scalar_tensor_tensor(x[:, b, at], y[:, b, j * C:(j + 1) * C], h[:, b, i, j:j + 1],
                                                 x[:, b, at], ALU.mult, ALU.add).then_inc(mixed, 1)


def gated_blocks(nc, io, out):
    scratch = {
        name: nc.dram_tensor(f"scratch_{name}", shape, F32, kind="Internal").ap()
        for name, shape in (
            ("k0", (G0, HD0, B, KEYS + S)), ("v0", (B, KR, KC, KV0)), ("v0x", (B, S, KV0)),
            ("k1", (G1, HD1, B, KEYS)), ("v1", (B, KR, KC, KV1)))
    }
    project_context_layer1(nc, io, scratch)
    with ExitStack() as stack:
        sb, _, _ = allocators(nc, stack, "stream")
        tokens = sb("tokens", [P, NC, T])
        with ExitStack() as inner:
            sb, _, _ = allocators(nc, inner, "normed")
            ln_hi = sb("hi", [P, NC, T], F32R)
            ln_lo = sb("lo", [P, NC, T], F32R)
            layer_norm(nc, io, "norm0", tokens, ln_hi, ln_lo, load=True)
            project_layer0(nc, io, scratch, ln_hi, ln_lo)
            attend(nc, io, scratch, tokens, ln_hi, ln_lo, 0)
            layer_norm(nc, io, "norm1", tokens, ln_hi, ln_lo)
            feed_forward(nc, io, tokens, ln_hi, ln_lo)
            layer_norm(nc, io, "norm2", tokens, ln_hi, ln_lo)
            attend(nc, io, scratch, tokens, ln_hi, ln_lo, 1)
        mix_streams(nc, io, tokens, out)


def lay_out(a):
    import numpy as np

    def chunks(w):
        return np.ascontiguousarray(w.T).reshape(-1, P, w.shape[0])

    def tiles(w, n):
        return w.reshape(-1, n, w.shape[1] // P, P).transpose(0, 3, 2, 1).reshape(-1, P, w.shape[1] // P * n)

    def out_tiles(w, groups, width):
        return w.reshape(4, D // 4, groups, HG, width).transpose(2, 0, 4, 3, 1).reshape(groups * 4, width, D)

    ctx = np.zeros((B, P, NC, CW), np.float32)
    ctx[..., :KEYS] = a["ctx_4096"].transpose(0, 2, 1).reshape(B, NC, P, KEYS).transpose(0, 2, 1, 3)

    def spread(g, rows):
        return np.tile(g.reshape(-1, 1, 1), (1, rows, 1))

    return {
        "ctxT": ctx,
        "xT": a["x"].reshape(T, NC, P).transpose(2, 1, 0),
        "mask": a["mask_1x1xSxS2_ff0"].reshape(S, KEYS),
        "gx": spread(a["g_xattn"], P),
        "gf": spread(a["g_ffn"][0:1], P),
        "gates": np.concatenate([spread(a["g_ffn"][1:2], S)[0], spread(a["L1_ffn_gate"], S)[0]], axis=1),
        "wk0T": chunks(a["L0_xattn_Wk"]),
        "wv0T": chunks(a["L0_xattn_Wv"]),
        "wk1T": chunks(a["L1_xattn_Wk"]),
        "wv1T": chunks(a["L1_xattn_Wv"]),
        "wq0": tiles(a["L0_xattn_Wq"], HD0),
        "wq1": tiles(a["L1_xattn_Wq"], HD1),
        "wo0": out_tiles(a["L0_xattn_Wo"], G0, HD0),
        "wo1": out_tiles(a["L1_xattn_Wo"], G1, HD1),
        "qn": a["L1_xattn_q_norm_w"].reshape(P, 1),
        "kn": a["L1_xattn_k_norm_w"].reshape(P, 1),
        "wf": tiles(np.concatenate([a["L0_ffn_Wq"], a["L0_ffn_Wk"], a["L0_ffn_A"].reshape(P, D), a["L0_ffn_W"]]), P),
        "bmT": a["L0_ffn_Bm"].transpose(0, 2, 1).reshape(P, D),
        "bT": a["L0_ffn_b"].reshape(NC, P).T,
        "wm": np.concatenate([a["L1_ffn_W_res"], a["L1_ffn_W_pre"], a["L1_ffn_W_post"]]).reshape(-1, NC, P).transpose(2, 1, 0),
        "branch": a["L1_ffn_W_branch"].reshape(-1, P, D // 4).transpose(1, 0, 2),
        "base": np.tile(np.concatenate([a["L1_ffn_H_res_base"].reshape(-1), a["L1_ffn_H_pre_base"],
                                        a["L1_ffn_H_post_base"]]), (S, 1)),
    }


def kernel(**inputs):
    import numpy as np
    import concourse.bacc as bacc
    from concourse.bass_utils import run_bass_kernel_spmd

    nc = bacc.Bacc("TRN2", target_bir_lowering=False, num_devices=1)
    arrays, io = {}, {}
    for name, value in lay_out({k: np.asarray(v) for k, v in inputs.items()}).items():
        value = np.ascontiguousarray(value)
        arrays[f"in_{name}"] = value
        io[name] = nc.dram_tensor(f"in_{name}", value.shape, F32, kind="ExternalInput").ap()
    out = nc.dram_tensor("out", (B, S, D), F32, kind="ExternalOutput").ap()
    gated_blocks(nc, io, out)
    result = run_bass_kernel_spmd(nc, [arrays], core_ids=[0])
    return result.results[0]["out"]
```
